# Optimizing a Trainium2 kernel written in Bass

```python
import numpy as np
import jax
import jax.numpy as jnp

def _softmax(x, axis=-1):
    return jax.nn.softmax(x, axis=axis)

def _gelu(x):
    return jax.nn.gelu(x, approximate=True)

def _silu(x):
    return jax.nn.silu(x)

def _sigmoid(x):
    return jax.nn.sigmoid(x)

def _layernorm(x, axis=-1, eps=1e-05):
    m = jnp.mean(x, axis=axis, keepdims=True)
    v = jnp.var(x, axis=axis, keepdims=True)
    return (x - m) / jnp.sqrt(v + eps)

def _scatter_add(tgt, idx, src, axis=0):
    return tgt.at[idx].add(src)

def _segment_sum(src, seg, n):
    return jax.ops.segment_sum(src, seg, n)
kernel_name = 'mk_adj_ffn_d1_adj_r2_69e2d6'

def setup_inputs(seed: int=0):
    np.random.seed(seed)
    _w = jnp.asarray

    def _rec_inputs():
        import jax
        import jax.numpy as jnp
        _gk = jax.random.key(seed)
        x = -0.0002928 + 1 * jax.random.normal(jax.random.fold_in(_gk, 1), (8, 1024, 256), jnp.float32)
        _a = jax.random.bernoulli(jax.random.fold_in(_gk, 2), 0.00195312, (8, 1024, 1024))
        adj = _a.astype(jnp.int32)
        return (x, adj)
    x, adj = _rec_inputs()

    def _L0_gnn_setup():
        import jax, jax.numpy as jnp
        import numpy as np
        L = 3
        D = 256
        B, N = (8, 512)
        EPS = 1e-05

        def layernorm(x, gamma, beta):
            mu = jnp.mean(x, axis=-1, keepdims=True)
            var = jnp.var(x, axis=-1, keepdims=True)
            return (x - mu) * jax.lax.rsqrt(var + EPS) * gamma + beta
        key = jax.random.key(seed)
        ks = jax.random.split(key, 12)
        s = 1.0 / np.sqrt(D)
        node_features = jax.random.normal(ks[0], (B, N, D), dtype=jnp.float32)
        adjacency_matrix = jax.random.randint(ks[1], (B, N, N), 0, 2, dtype=jnp.int32)
        return {'node_features': node_features, 'adjacency_matrix': adjacency_matrix, 'attn_w': jax.random.normal(ks[2], (L, 2 * D), dtype=jnp.float32) * (1.0 / np.sqrt(2 * D)), 'attn_b': jax.random.normal(ks[3], (L,), dtype=jnp.float32) * 0.01, 'W1': jax.random.normal(ks[4], (L, D, 4 * D), dtype=jnp.float32) * s, 'b1': jnp.zeros((L, 4 * D), dtype=jnp.float32), 'W2': jax.random.normal(ks[5], (L, 4 * D, D), dtype=jnp.float32) * (1.0 / np.sqrt(4 * D)), 'b2': jnp.zeros((L, D), dtype=jnp.float32), 'g1': jnp.ones((L, D), dtype=jnp.float32), 'beta1': jnp.zeros((L, D), dtype=jnp.float32), 'g2': jnp.ones((L, D), dtype=jnp.float32), 'beta2': jnp.zeros((L, D), dtype=jnp.float32)}
    _L0_gnn_all = _L0_gnn_setup()
    _L0_gnn_in = {k: v for k, v in _L0_gnn_all.items() if k in ('attn_w', 'attn_b', 'W1', 'b1', 'W2', 'b2', 'g1', 'beta1', 'g2', 'beta2')}
    del _L0_gnn_all

    def _L0_ffn_setup():
        import jax, jax.numpy as jnp
        import numpy as np
        MICRO_BATCHES = 2
        TOP_K = 2
        D = 256
        E = 8
        B, S = (8, 4096)
        key = jax.random.key(seed)
        ks = jax.random.split(key, 12)
        s = 0.02
        return {'x': jax.random.normal(ks[0], (B, S, D), dtype=jnp.float32), 'ln_g': jnp.ones((D,), jnp.float32), 'ln_b': jnp.zeros((D,), jnp.float32), 'attn_w': jax.random.normal(ks[1], (D, D), jnp.float32) * s, 'attn_b': jnp.zeros((D,), jnp.float32), 'gate_w': jax.random.normal(ks[2], (E, D), jnp.float32) * s, 'fc1_w': jax.random.normal(ks[3], (E, 4 * D, D), jnp.float32) * s, 'fc1_b': jnp.zeros((E, 4 * D), jnp.float32), 'fc2_w': jax.random.normal(ks[4], (E, D, 4 * D), jnp.float32) * s, 'fc2_b': jnp.zeros((E, D), jnp.float32), 'next_w': jax.random.normal(ks[5], (D, D), jnp.float32) * s, 'next_b': jnp.zeros((D,), jnp.float32)}
    _L0_ffn_all = _L0_ffn_setup()
    _L0_ffn_in = {k: v for k, v in _L0_ffn_all.items() if k in ('ln_g', 'ln_b', 'attn_w', 'attn_b', 'gate_w', 'fc1_w', 'fc1_b', 'fc2_w', 'fc2_b', 'next_w', 'next_b')}
    del _L0_ffn_all
    return {'x': x, 'adj': adj, 'L0_gnn_attn_w': _L0_gnn_in['attn_w'], 'L0_gnn_attn_b': _L0_gnn_in['attn_b'], 'L0_gnn_W1': _L0_gnn_in['W1'], 'L0_gnn_b1': _L0_gnn_in['b1'], 'L0_gnn_W2': _L0_gnn_in['W2'], 'L0_gnn_b2': _L0_gnn_in['b2'], 'L0_gnn_g1': _L0_gnn_in['g1'], 'L0_gnn_beta1': _L0_gnn_in['beta1'], 'L0_gnn_g2': _L0_gnn_in['g2'], 'L0_gnn_beta2': _L0_gnn_in['beta2'], 'L0_ffn_ln_g': _L0_ffn_in['ln_g'], 'L0_ffn_ln_b': _L0_ffn_in['ln_b'], 'L0_ffn_attn_w': _L0_ffn_in['attn_w'], 'L0_ffn_attn_b': _L0_ffn_in['attn_b'], 'L0_ffn_gate_w': _L0_ffn_in['gate_w'], 'L0_ffn_fc1_w': _L0_ffn_in['fc1_w'], 'L0_ffn_fc1_b': _L0_ffn_in['fc1_b'], 'L0_ffn_fc2_w': _L0_ffn_in['fc2_w'], 'L0_ffn_fc2_b': _L0_ffn_in['fc2_b'], 'L0_ffn_next_w': _L0_ffn_in['next_w'], 'L0_ffn_next_b': _L0_ffn_in['next_b']}

def reference(x, adj, L0_gnn_attn_w, L0_gnn_attn_b, L0_gnn_W1, L0_gnn_b1, L0_gnn_W2, L0_gnn_b2, L0_gnn_g1, L0_gnn_beta1, L0_gnn_g2, L0_gnn_beta2, L0_ffn_ln_g, L0_ffn_ln_b, L0_ffn_attn_w, L0_ffn_attn_b, L0_ffn_gate_w, L0_ffn_fc1_w, L0_ffn_fc1_b, L0_ffn_fc2_w, L0_ffn_fc2_b, L0_ffn_next_w, L0_ffn_next_b):
    import jax
    import jax.numpy as jnp

    def _L0_gnn_ref(node_features, adjacency_matrix, attn_w, attn_b, W1, b1, W2, b2, g1, beta1, g2, beta2):
        import jax, jax.numpy as jnp
        import numpy as np
        L = 3
        D = 256
        B, N = (8, 512)
        EPS = 1e-05

        def layernorm(x, gamma, beta):
            mu = jnp.mean(x, axis=-1, keepdims=True)
            var = jnp.var(x, axis=-1, keepdims=True)
            return (x - mu) * jax.lax.rsqrt(var + EPS) * gamma + beta
        n = adjacency_matrix.shape[-1]
        mask = adjacency_matrix.astype(jnp.float32) + jnp.eye(n, dtype=jnp.float32) > 0
        x = node_features
        d = x.shape[-1]
        for l in range(attn_w.shape[0]):
            si = x @ attn_w[l, :d]
            sj = x @ attn_w[l, d:]
            scores = si[:, :, None] + sj[:, None, :] + attn_b[l]
            scores = jnp.where(scores >= 0, scores, 0.2 * scores)
            scores = jnp.where(mask, scores, -jnp.inf)
            attn = jax.nn.softmax(scores, axis=-1)
            agg = jnp.einsum('bij,bjd->bid', attn, x)
            h = layernorm(x + agg, g1[l], beta1[l])
            ff = jax.nn.gelu(h @ W1[l] + b1[l], approximate=False) @ W2[l] + b2[l]
            x = layernorm(h + ff, g2[l], beta2[l])
        return x

    def _L0_ffn_ref(x, ln_g, ln_b, attn_w, attn_b, gate_w, fc1_w, fc1_b, fc2_w, fc2_b, next_w, next_b):
        import jax, jax.numpy as jnp
        import numpy as np
        MICRO_BATCHES = 2
        TOP_K = 2
        D = 256
        E = 8
        B, S = (8, 4096)
        b, s, d = x.shape
        xf = x.reshape(b * s, d)
        mu = jnp.mean(xf, axis=-1, keepdims=True)
        var = jnp.var(xf, axis=-1, keepdims=True)
        normed = (xf - mu) / jnp.sqrt(var + 1e-05) * ln_g + ln_b
        x_attn = normed @ attn_w.T + attn_b + xf
        logits = x_attn @ gate_w.T
        _scores, _indices = jax.lax.top_k(logits, TOP_K)
        e = fc1_w.shape[0]
        t = b * s // (MICRO_BATCHES * e)
        tok = x_attn.reshape(MICRO_BATCHES, e, t, d)
        h = jnp.einsum('meti,ehi->meth', tok, fc1_w) + fc1_b[None, :, None, :]
        h = jax.nn.gelu(h, approximate=False)
        y = jnp.einsum('meth,edh->metd', h, fc2_w) + fc2_b[None, :, None, :]
        yf = y.reshape(b * s, d)
        out = jax.nn.gelu(yf @ next_w.T + next_b, approximate=False)
        return out.reshape(b, s, d)
    x = x + _L0_gnn_ref(_layernorm(x, axis=-1), adj, L0_gnn_attn_w, L0_gnn_attn_b, L0_gnn_W1, L0_gnn_b1, L0_gnn_W2, L0_gnn_b2, L0_gnn_g1, L0_gnn_beta1, L0_gnn_g2, L0_gnn_beta2)
    x = x + _L0_ffn_ref(_layernorm(x, axis=-1), L0_ffn_ln_g, L0_ffn_ln_b, L0_ffn_attn_w, L0_ffn_attn_b, L0_ffn_gate_w, L0_ffn_fc1_w, L0_ffn_fc1_b, L0_ffn_fc2_w, L0_ffn_fc2_b, L0_ffn_next_w, L0_ffn_next_b)
    return x

_drawn_inputs = setup_inputs


def setup_inputs(seed=0):
    import zlib

    import numpy as np

    out = dict(_drawn_inputs(seed))
    spreads = {'L0_gnn_b1': (0.0, 0.1),
     'L0_gnn_b2': (0.0, 0.1),
     'L0_gnn_g1': (1.0, 0.2),
     'L0_gnn_beta1': (0.0, 0.1),
     'L0_gnn_g2': (1.0, 0.2),
     'L0_gnn_beta2': (0.0, 0.1),
     'L0_ffn_ln_g': (1.0, 0.6),
     'L0_ffn_ln_b': (0.0, 0.8),
     'L0_ffn_attn_b': (0.0, 0.8),
     'L0_ffn_fc1_b': (0.0, 0.8),
     'L0_ffn_fc2_b': (0.0, 0.8),
     'L0_ffn_next_b': (0.0, 0.8)}
    factors = {'L0_gnn_attn_b': 64.0,
     'L0_ffn_attn_w': 8.0,
     'L0_ffn_fc1_w': 4.951,
     'L0_ffn_fc2_w': 4.646,
     'L0_ffn_next_w': 3.646}
    for name, (base, spread) in spreads.items():
        noise = np.random.default_rng([zlib.crc32(name.encode()), seed]).standard_normal(out[name].shape)
        drawn = base * np.exp(spread * noise) if base else spread * noise
        out[name] = jnp.asarray(drawn.astype(out[name].dtype))
    for name, factor in factors.items():
        out[name] = (out[name] * factor).astype(out[name].dtype)
    return out
```

```python
from contextlib import ExitStack

import concourse.bass as bass
from concourse import mybir

P = 128
F32 = mybir.dt.float32
BF16 = mybir.dt.bfloat16
I32 = mybir.dt.int32
U8 = mybir.dt.uint8
ALU = mybir.AluOpType
ACT = mybir.ActivationFunctionType
AX = mybir.AxisListType


def adj_ffn_kernel(nc, x, adj, adj_t, attn_rows, attn_b, w1, b1, w2, rows, ffn_cols, attn_w, fc1, fc2, expert_cols,
                   next_w, next_b, eye, out):
    B, _, NT, D = x.shape
    N = NT * P
    L = w1.shape[0]
    KD = D // P
    HID = w1.shape[3]
    KH = HID // P
    PAIRS = B // 2
    UR = 4
    U = UR * P
    HALVES = NT // UR
    EPS = 1e-5
    SLOPE = 0.2

    GNN = L * 2 * HALVES
    FFN = 2 * HALVES
    UNITS = GNN + FFN
    PREPS = L * 2
    S_TILES = N // U
    WORK = PREPS * S_TILES + GNN * (KD + KH) + FFN * (2 * KD + KH)
    AGG = GNN * UR + FFN * (KD + UR)
    HIDS = UNITS * KH
    PT = GNN * NT
    ADJS = PREPS * NT
    WORK_BUFS, AGG_BUFS, HID_BUFS, ADJ_BUFS = 2, 2, 4, 2
    W_SLOTS = 3
    STAGES = L + HALVES

    def unit(g):
        return g // (2 * HALVES), g // HALVES % 2, g % HALVES

    S_AT = KH // 2

    def prep_after(g):
        l, b, half = unit(g)
        if half == 0 and b == 1 and l + 1 < L:
            return 2 * (l + 1)
        if half == 0 and b == 0 and l > 0:
            return 2 * l + 1
        return None

    s_tile_end, hT_end, front_end = {0: S_TILES, 1: 2 * S_TILES}, {}, {}
    tiles = 2 * S_TILES
    for g in range(GNN):
        hT_end[g] = tiles + KD
        if prep_after(g) is not None:
            s_tile_end[prep_after(g)] = tiles + KD + S_AT + 2 + S_TILES
            tiles += S_TILES
        tiles += KD + KH
    for f in range(FFN):
        if f == 0:
            tiles += 2 * KD
        front_end[f] = tiles
        tiles += KH + (2 * KD if f + 1 < FFN else 0)
    assert tiles == WORK

    with ExitStack() as ctx:
        def sb(name, shape, dt=F32):
            return ctx.enter_context(nc.sbuf_tensor(name, shape, dt))

        def sem(name):
            return ctx.enter_context(nc.semaphore(name))

        X = [sb(f"X{i}", [P, NT, D + 1]) for i in range(2)]
        mask = [sb(f"mask{i}", [P, NT, N], U8) for i in range(2)]
        prob = sb("prob", [P, 2, NT, U])
        branch = sb("branch", [P, NT, U])
        hid = sb("hid", [P, HID_BUFS, U])
        w1s = sb("w1s", [P, W_SLOTS, KD, HID])
        w2s = sb("w2s", [P, W_SLOTS, KH, D])
        h = sb("h", [P, UR, D])
        e = sb("e", [P, 2, UR, D])
        hT = sb("hT", [P, KD, U])
        s_row = sb("s_row", [P, N])
        adj_rows = sb("adj_rows", [P, ADJ_BUFS, N], I32)
        junk = sb("junk", [P, N], BF16)
        row_s = sb("row_s", [P, L, 5, D])
        attn_row = sb("attn_row", [P, L, 2, D])
        attn_bias = sb("attn_bias", [P, L])
        b1s = sb("b1s", [P, L, KH])
        ffn_col = sb("ffn_col", [P, 3, KD])
        exp_col = sb("exp_col", [P, HALVES, KH + KD])
        attn_ws = sb("attn_ws", [P, KD, D])
        next_ws = sb("next_ws", [P, KD, D])
        next_row = sb("next_row", [P, D])
        ident = sb("ident", [P, P])
        ident8 = sb("ident8", [P, P], U8)
        si = sb("si", [P, 2, NT])
        sj = sb("sj", [P, 2, NT])
        sj2 = sb("sj2", [P, 2, NT])
        G = sb("G", [P, 2, NT])
        H = sb("H", [P, 2, NT])
        c_col = sb("c_col", [P, NT])
        m_col = sb("m_col", [P, NT])
        u_col = sb("u_col", [P, NT])
        smin = sb("smin", [P, 1])
        rden = sb("rden", [P, UR, 1])
        stats = sb("stats", [P, NT, 6])
        mv = sb("mv", [P, NT, 2])
        var_e = sb("var_e", [P, NT])
        rstd = sb("rstd", [P, NT])
        neg_half = sb("neg_half", [P, NT])
        eps_row = sb("eps_row", [P, NT])

        xfT = prob[:, 0, 0:KD, :]
        nT = prob[:, 0, KD:2 * KD, :]
        yT = prob[:, 0, 2 * KD:3 * KD, :]
        x_in = branch[:, :, :].rearrange("p (f a) (b d) -> p f (a b) d", f=FFN, d=D)

        agg = [ctx.enter_context(nc.psum_tensor(f"agg{i}", [P, 512], F32)) for i in range(2)]
        ff = [ctx.enter_context(nc.psum_tensor(f"ff{i}", [P, 512], F32)) for i in range(2)]
        work = [ctx.enter_context(nc.psum_tensor(f"work{i}", [P, 512], F32)) for i in range(2)]
        g_bc = ctx.enter_context(nc.psum_tensor("g_bc", [P, 512], F32))
        h_bc = ctx.enter_context(nc.psum_tensor("h_bc", [P, 512], F32))

        consts_in = sem("consts_in")
        ident8_in = sem("ident8_in")
        x_loaded = sem("x_loaded")
        xin_loaded = sem("xin_loaded")
        mask_loaded = sem("mask_loaded")
        adj_loaded = [sem(f"adj_loaded{i}") for i in range(ADJ_BUFS)]
        w_loaded = [sem(f"w_loaded{i}") for i in range(STAGES)]
        stored = sem("stored")
        work_done = sem("work_done")
        work_moved = sem("work_moved")
        agg_done = sem("agg_done")
        agg_moved = sem("agg_moved")
        hid_used = sem("hid_used")
        ff_moved = sem("ff_moved")
        bcast_done = sem("bcast_done")
        exps_done = sem("exps_done")
        prob_ready = sem("prob_ready")
        s_ready = sem("s_ready")
        cols_ready = sem("cols_ready")
        adj_used = sem("adj_used")
        h_ready = sem("h_ready")
        var_ready = sem("var_ready")
        rstd_ready = sem("rstd_ready")
        hb_ready = sem("hb_ready")
        z_ready = sem("z_ready")
        x_ready = sem("x_ready")
        front_ready = sem("front_ready")
        o_gelu = sem("o_gelu")
        y_ready = sem("y_ready")
        dve_step = sem("dve_step")
        pool_step = sem("pool_step")
        norm_consts = sem("norm_consts")
        ones_set = sem("ones_set")

        block = ctx.enter_context(nc.Block())

        NORMS = 2 + GNN * (UR + 1) + FFN * 2

        @block.sync
        def _(sp):
            for dst, src in ((row_s[:], rows.partition_broadcast(P)), (attn_row[:], attn_rows.partition_broadcast(P)),
                             (attn_bias[:], attn_b.partition_broadcast(P)), (b1s[:], b1), (ffn_col[:], ffn_cols),
                             (attn_ws[:], attn_w), (next_ws[:], next_w), (next_row[:], next_b.partition_broadcast(P)),
                             (ident[:], eye)):
                sp.dma_start(dst, src).then_inc(consts_in, 16)
            sp.sem_inc(stored, 16)
            with sp.Fori(0, PAIRS) as p:
                def load_w(s):
                    slot = s % W_SLOTS
                    if s >= L:
                        sp.wait_ge(hid_used, p * HIDS + (s - L + 1) * 2 * HALVES * KH + HID_BUFS)
                    if s < L:
                        sp.dma_start(w1s[:, slot], w1[s]).then_inc(w_loaded[s], 16)
                        sp.dma_start(w2s[:, slot], w2[s]).then_inc(w_loaded[s], 16)
                    else:
                        j = p * HALVES + (s - L)
                        sp.dma_start(w1s[:, slot:slot + 1], fc1[bass.ds(j, 1)].rearrange("e p k n -> p e k n")).then_inc(w_loaded[s], 16)
                        sp.dma_start(w2s[:, slot:slot + 1], fc2[bass.ds(j, 1)].rearrange("e p k n -> p e k n")).then_inc(w_loaded[s], 16)
                        sp.dma_start(exp_col[:, s - L:s - L + 1], expert_cols[bass.ds(j, 1)].rearrange("e p n -> p e n")).then_inc(w_loaded[s], 16)

                def load_adj(k):
                    b = k % 2
                    for t in range(NT):
                        n = k * NT + t
                        sp.wait_ge(adj_used, p * ADJS + n + 1)
                        sp.dma_start(adj_rows[:, n % ADJ_BUFS:n % ADJ_BUFS + 1],
                                     adj[bass.ds(p + b * PAIRS, 1), t * P:(t + 1) * P, :].rearrange("o p n -> p o n"))\
                            .then_inc(adj_loaded[n % ADJ_BUFS], 16)

                sp.wait_ge(stored, p * FFN * 16 + 16)
                for b in range(2):
                    sp.dma_start(X[b][:, :, 0:D], x[bass.ds(p + b * PAIRS, 1)].rearrange("o p t d -> p (o t) d"))\
                        .then_inc(x_loaded, 16)
                load_w(0)
                load_adj(0)
                load_adj(1)
                load_w(1)
                load_w(2)
                load_adj(2)
                load_adj(3)
                load_w(3)
                load_adj(4)
                load_adj(5)
                load_w(4)
                sp.wait_ge(prob_ready, p * PT + PT)
                for f in range(FFN):
                    b, half = f % 2, f // 2
                    sp.dma_start(x_in[:, f], x[bass.ds(p + b * PAIRS, 1), :, half * UR:(half + 1) * UR, :]
                                 .rearrange("o p t d -> p (o t) d")).then_inc(xin_loaded, 16)
                for f in range(FFN):
                    b, half = f % 2, f // 2
                    sp.wait_ge(y_ready, p * FFN * UR + (f + 1) * UR)
                    sp.dma_start(out[bass.ds(p + b * PAIRS, 1), :, half * UR:(half + 1) * UR, :]
                                 .rearrange("o p t d -> p (o t) d"), e[:, 1]).then_inc(stored, 16)
            sp.wait_ge(stored, PAIRS * FFN * 16 + 16)

        @block.gpsimd
        def _(pool):
            pool.memset(neg_half[:], -0.5).then_inc(norm_consts, 1)
            pool.memset(eps_row[:], EPS).then_inc(norm_consts, 1)
            pool.wait_ge(norm_consts, 2)
            pool.dma_start(ident8[:], eye).then_inc(ident8_in, 16)
            pool.wait_ge(consts_in, 144)
            with pool.Fori(0, PAIRS) as p:
                pool.sem_clear(pool_step)
                steps = [0]
                norms = [0]

                for b in range(2):
                    pool.dma_start(mask[b][:], adj_t[bass.ds(p + b * PAIRS, 1)].rearrange("o p t n -> p (o t) n"))\
                        .then_inc(mask_loaded, 16)

                def step(ins):
                    steps[0] += 1
                    ins.then_inc(pool_step, 1)
                    return steps[0]

                def power(a, b):
                    pool.wait_ge(var_ready, p * NORMS + norms[0] + 1)
                    n = step(pool.tensor_tensor(var_e[:, a:b], mv[:, a:b, 1], eps_row[:, a:b], ALU.add))
                    pool.wait_ge(pool_step, n)
                    pool.tensor_tensor(rstd[:, a:b], var_e[:, a:b], neg_half[:, a:b], ALU.pow).then_inc(rstd_ready, 1)
                    norms[0] += 1

                def first_power(g):
                    for r in range(UR):
                        power(r, r + 1)

                def add_b2(g):
                    for r in range(UR):
                        pool.wait_ge(h_ready, p * GNN * UR + g * UR + r + 1)
                        pool.tensor_tensor(e[:, g % 2, r], h[:, r], row_s[:, unit(g)[0], 0], ALU.add).then_inc(hb_ready, 1)

                def affine(g):
                    l, b, half = unit(g)
                    for r in range(UR):
                        pool.wait_ge(z_ready, p * GNN * UR + g * UR + r + 1)
                        n = step(pool.tensor_tensor(e[:, g % 2, r], e[:, g % 2, r], row_s[:, l, 3], ALU.mult))
                        pool.wait_ge(pool_step, n)
                        pool.tensor_tensor(X[b][:, half * UR + r, 0:D], e[:, g % 2, r], row_s[:, l, 4], ALU.add)\
                            .then_inc(x_ready, 1)

                power(0, NT)
                power(0, NT)
                for g in range(GNN):
                    if g >= 1:
                        power(UR, 2 * UR)
                    first_power(g)
                    add_b2(g)
                    if g >= 1:
                        affine(g - 1)
                power(0, UR)
                power(0, UR)
                power(UR, 2 * UR)
                affine(GNN - 1)
                for f in range(FFN):
                    if f + 1 < FFN:
                        power(0, UR)
                        power(0, UR)
                    b, half = f % 2, f // 2
                    for r in range(UR):
                        pool.wait_ge(o_gelu, p * FFN * UR + f * UR + r + 1)
                        pool.tensor_tensor(e[:, 1, r], e[:, 1, r], X[b][:, half * UR + r, 0:D], ALU.add).then_inc(y_ready, 1)

        @block.vector
        def _(dve):
            for b in range(2):
                dve.memset(X[b][:, :, D:D + 1], 1.0).then_inc(ones_set, 1)
            dve.sem_inc(agg_moved, AGG_BUFS)
            dve.sem_inc(ff_moved, 1)
            dve.sem_inc(adj_used, ADJ_BUFS)
            dve.wait_ge(consts_in, 144)
            dve.wait_ge(ident8_in, 16)
            dve.wait_ge(ones_set, 2)
            with dve.Fori(0, PAIRS) as p:
                dve.sem_clear(dve_step)
                steps = [0]
                norms = [0]
                aggs = [0]

                def step(ins):
                    steps[0] += 1
                    ins.then_inc(dve_step, 1)
                    return steps[0]

                def need(n):
                    dve.wait_ge(dve_step, n)

                def ask_rstd(tiles):
                    ns = [step(dve.bn_stats(stats[:, t, :], src)) for t, src in tiles]
                    for (t, _), n in zip(tiles, ns):
                        need(n)
                        ins = dve.bn_aggr(mv[:, t, :], stats[:, t, :])
                    ins.then_inc(var_ready, 1)
                    norms[0] += 1
                    return norms[0]

                def normalise(dst, src, t):
                    return dve.tensor_scalar(dst, src, mv[:, t, 0:1], rstd[:, t:t + 1], ALU.subtract, ALU.mult)

                def dots(l, b, t, before):
                    if before is not None:
                        need(before)
                    for which, col in ((0, si), (1, sj)):
                        n = step(dve.tensor_tensor_reduce(junk[:, which * D:(which + 1) * D], X[b][:, t, 0:D], attn_row[:, l, which],
                                                          1.0, 0.0, ALU.mult, ALU.add, col[:, b, t:t + 1]))
                    return n

                def prepare(k):
                    l, b = k // 2, k % 2
                    dve.wait_ge(work_moved, p * WORK + s_tile_end[k] + WORK_BUFS)
                    need(step(dve.tensor_reduce(smin[:], s_row[:], AX.X, ALU.min)))
                    step(dve.tensor_scalar(s_row[:], s_row[:], smin[:], 1.0, ALU.subtract, ALU.add))
                    for t in range(NT):
                        n = k * NT + t
                        dve.wait_ge(adj_used, p * ADJS + n + ADJ_BUFS)
                        dve.wait_ge(adj_loaded[n % ADJ_BUFS], (p * ADJS + n - n % ADJ_BUFS) * (16 // ADJ_BUFS) + 16)
                        need(step(dve.memset(u_col[:, t:t + 1], 0.0)))
                        dve.tensor_tensor_reduce(junk[:], adj_rows[:, n % ADJ_BUFS], s_row[:], 1.0, 0.0, ALU.mult, ALU.max,
                                                 u_col[:, t:t + 1]).then_inc(adj_used, 1)
                    dve.wait_ge(adj_used, p * ADJS + (k + 1) * NT + ADJ_BUFS)
                    need(step(dve.tensor_scalar(u_col[:], u_col[:], -1.0, smin[:], ALU.add, ALU.add)))
                    need(step(dve.tensor_tensor(u_col[:], u_col[:], sj[:, b], ALU.max)))
                    need(step(dve.tensor_scalar(c_col[:], si[:, b], attn_bias[:, l:l + 1], None, ALU.add)))
                    need(step(dve.tensor_tensor(u_col[:], u_col[:], c_col[:], ALU.add)))
                    need(step(dve.scalar_tensor_tensor(m_col[:], u_col[:], SLOPE, u_col[:], ALU.mult, ALU.max)))
                    step(dve.tensor_tensor(G[:, b], c_col[:], m_col[:], ALU.subtract))
                    step(dve.tensor_scalar(sj2[:, b], sj[:, b], SLOPE, None, ALU.mult))
                    dve.scalar_tensor_tensor(H[:, b], c_col[:], SLOPE, m_col[:], ALU.mult, ALU.subtract).then_inc(cols_ready, 1)

                def probabilities(g):
                    l, b, half = unit(g)
                    for t in range(NT):
                        dve.wait_ge(exps_done, p * PT + g * NT + t + 1)
                        need(step(dve.tensor_tensor(prob[:, g % 2, t], prob[:, g % 2, t], branch[:, t], ALU.max)))
                        dve.tensor_tensor(prob[:, g % 2, t], prob[:, g % 2, t], mask[b][:, t, half * U:(half + 1) * U], ALU.min)\
                            .then_inc(prob_ready, 1)

                def first_norm(g):
                    l, b, half = unit(g)
                    for r in range(UR):
                        bank = agg[aggs[0] % AGG_BUFS]
                        dve.wait_ge(agg_done, p * AGG + aggs[0] + 1)
                        need(step(dve.reciprocal(rden[:, r], bank[:, D:D + 1])))
                        dve.scalar_tensor_tensor(h[:, r], bank[:, 0:D], rden[:, r], X[b][:, half * UR + r, 0:D], ALU.mult, ALU.add)\
                            .then_inc(agg_moved, 1)
                        aggs[0] += 1
                        dve.wait_ge(agg_moved, p * AGG + aggs[0] + AGG_BUFS)
                        asked = ask_rstd([(r, h[:, r])])
                        dve.wait_ge(rstd_ready, p * NORMS + asked)
                        need(step(normalise(h[:, r], h[:, r], r)))
                        need(step(dve.tensor_tensor(h[:, r], h[:, r], row_s[:, l, 1], ALU.mult)))
                        dve.tensor_tensor(h[:, r], h[:, r], row_s[:, l, 2], ALU.add).then_inc(h_ready, 1)

                def second_sums(g):
                    dve.wait_ge(hid_used, p * HIDS + (g + 1) * KH + HID_BUFS)
                    dve.wait_ge(hb_ready, p * GNN * UR + (g + 1) * UR)
                    for r in range(UR):
                        ins = dve.tensor_tensor(e[:, g % 2, r], ff[r // 2][:, r % 2 * D:(r % 2 + 1) * D], e[:, g % 2, r], ALU.add)
                        if r < UR - 1:
                            step(ins)
                    ins.then_inc(ff_moved, 1)
                    dve.wait_ge(ff_moved, p * UNITS + g + 2)
                    return ask_rstd([(UR + r, e[:, g % 2, r]) for r in range(UR)])

                def second_norm(g, asked):
                    l, b, half = unit(g)
                    dve.wait_ge(rstd_ready, p * NORMS + asked)
                    for r in range(UR):
                        normalise(e[:, g % 2, r], e[:, g % 2, r], UR + r).then_inc(z_ready, 1)
                    if l + 1 < L:
                        n = None
                        for r in range(UR):
                            dve.wait_ge(x_ready, p * GNN * UR + g * UR + r + 1)
                            n = dots(l + 1, b, half * UR + r, n)
                        if half == HALVES - 1:
                            need(n)
                            dve.tensor_scalar(sj2[:, b], sj[:, b], SLOPE, None, ALU.mult).then_inc(s_ready, 1)
                            dve.wait_ge(s_ready, p * PREPS + (l + 1) * 2 + b + 1)

                def front(f):
                    b, half = f % 2, f // 2
                    a = half * UR
                    l_unit = GNN - 2 * HALVES + b * HALVES + half
                    dve.wait_ge(x_ready, p * GNN * UR + max(l_unit + 1, GNN - 1) * UR)
                    dve.wait_ge(xin_loaded, p * FFN * 16 + FFN * 16)
                    need(step(dve.tensor_tensor(X[b][:, a:a + UR, 0:D], X[b][:, a:a + UR, 0:D], x_in[:, f], ALU.add)))
                    asked = ask_rstd([(r, X[b][:, a + r, 0:D]) for r in range(UR)])
                    dve.wait_ge(rstd_ready, p * NORMS + asked)
                    for r in range(UR):
                        n = step(normalise(h[:, r], X[b][:, a + r, 0:D], r))
                    need(n)
                    asked = ask_rstd([(r, h[:, r]) for r in range(UR)])
                    dve.wait_ge(rstd_ready, p * NORMS + asked)
                    for r in range(UR):
                        ins = normalise(e[:, 0, r], h[:, r], r)
                        if r < UR - 1:
                            step(ins)
                    ins.then_inc(front_ready, 1)

                dve.wait_ge(x_loaded, p * 32 + 32)
                for b in range(2):
                    asked = ask_rstd([(t, X[b][:, t, 0:D]) for t in range(NT)])
                    dve.wait_ge(rstd_ready, p * NORMS + asked)
                    for t in range(NT):
                        n = step(normalise(X[b][:, t, 0:D], X[b][:, t, 0:D], t))
                    need(n)
                    for t in range(NT):
                        n = dots(0, b, t, n)
                    need(n)
                    dve.tensor_scalar(sj2[:, b], sj[:, b], SLOPE, None, ALU.mult).then_inc(s_ready, 1)
                    dve.wait_ge(s_ready, p * PREPS + b + 1)
                dve.wait_ge(mask_loaded, p * 32 + 32)
                for b in range(2):
                    for t in range(NT):
                        own = mask[b][:, t, t * P:(t + 1) * P]
                        n = step(dve.tensor_tensor(own, own, ident8[:], ALU.add))
                need(n)
                prepare(0)
                prepare(1)
                probabilities(0)

                for g in range(GNN):
                    l, b, half = unit(g)
                    if g >= 1:
                        asked = second_sums(g - 1)
                    first_norm(g)
                    if g >= 1:
                        second_norm(g - 1, asked)
                    k = prep_after(g)
                    if k is not None:
                        prepare(k)
                    if g + 1 < GNN:
                        probabilities(g + 1)
                dve.wait_ge(work_done, p * WORK + hT_end[GNN - 1])
                dve.wait_ge(hb_ready, p * GNN * UR + GNN * UR)
                front(0)
                asked = second_sums(GNN - 1)
                second_norm(GNN - 1, asked)
                for f in range(FFN):
                    for d in range(KD):
                        dve.wait_ge(agg_done, p * AGG + aggs[0] + 1)
                        dve.wait_ge(work_moved, p * WORK + front_end[f] + WORK_BUFS)
                        dve.scalar_tensor_tensor(xfT[:, d], agg[aggs[0] % AGG_BUFS][:, 0:U], ffn_col[:, 2, d:d + 1], xfT[:, d],
                                                 ALU.add, ALU.add).then_inc(agg_moved, 1)
                        aggs[0] += 1
                    if f + 1 < FFN:
                        front(f + 1)
                    dve.wait_ge(hid_used, p * HIDS + (GNN + f + 1) * KH + HID_BUFS)
                    for d in range(KD):
                        ins = dve.tensor_scalar(yT[:, d], ff[d][:, 0:U], exp_col[:, f // 2, KH + d:KH + d + 1], None, ALU.add)
                        if d < KD - 1:
                            step(ins)
                    ins.then_inc(ff_moved, 1)
                    for r in range(UR):
                        dve.wait_ge(agg_done, p * AGG + aggs[0] + 1)
                        if r == 0 and f > 0:
                            dve.wait_ge(stored, p * FFN * 16 + f * 16 + 16)
                        dve.tensor_tensor(e[:, 1, r], agg[aggs[0] % AGG_BUFS][:, 0:D], next_row[:], ALU.add).then_inc(agg_moved, 1)
                        aggs[0] += 1
                dve.wait_ge(dve_step, steps[0])

        @block.scalar
        def _(act):
            act.sem_inc(work_moved, WORK_BUFS)
            act.wait_ge(consts_in, 144)
            with act.Fori(0, PAIRS) as p:
                works = [0]

                def branches(g):
                    l, b, half = unit(g)
                    act.wait_ge(bcast_done, p * GNN + g + 1)
                    if g >= 2:
                        act.wait_ge(agg_done, p * AGG + (g - 1) * UR)
                    for t in range(NT):
                        act.activation(prob[:, g % 2, t], g_bc[:, 0:U], ACT.Exp, bias=sj[:, b, t:t + 1])
                        if g >= 1:
                            act.wait_ge(prob_ready, p * PT + (g - 1) * NT + t + 1)
                        act.activation(branch[:, t], h_bc[:, 0:U], ACT.Exp, bias=sj2[:, b, t:t + 1]).then_inc(exps_done, 1)

                def move(dst, **how):
                    n = works[0]
                    act.wait_ge(work_done, p * WORK + n + 1)
                    act.activation(dst, work[n % WORK_BUFS][:, 0:U], **how).then_inc(work_moved, 1)
                    works[0] += 1

                def hidden(u, k, bias):
                    act.wait_ge(hid_used, p * HIDS + u * KH + k + 1)
                    move(hid[:, k % HID_BUFS], func=ACT.Gelu, bias=bias)

                def s_rows(k):
                    for t in range(S_TILES):
                        move(s_row[:, t * U:(t + 1) * U], func=ACT.Copy)

                s_rows(0)
                act.wait_ge(cols_ready, p * PREPS + 1)
                s_rows(1)
                branches(0)
                for g in range(GNN):
                    l, b, half = unit(g)
                    if g + 1 < GNN:
                        branches(g + 1)
                    for d in range(KD):
                        move(hT[:, d], func=ACT.Copy)
                    for k in range(KH):
                        hidden(g, k, b1s[:, l, k:k + 1])
                        if k == S_AT + 1 and prep_after(g) is not None:
                            act.wait_ge(cols_ready, p * PREPS + prep_after(g))
                            s_rows(prep_after(g))

                def front(f):
                    for d in range(KD):
                        move(xfT[:, d], func=ACT.Copy)
                    for d in range(KD):
                        move(nT[:, d], func=ACT.Identity, scale=ffn_col[:, 0, d:d + 1], bias=ffn_col[:, 1, d:d + 1])

                front(0)
                aggs = GNN * UR
                for f in range(FFN):
                    for k in range(KH):
                        hidden(GNN + f, k, exp_col[:, f // 2, k:k + 1])
                    if f + 1 < FFN:
                        front(f + 1)
                    aggs += KD
                    for r in range(UR):
                        aggs += 1
                        act.wait_ge(agg_moved, p * AGG + aggs + AGG_BUFS)
                        act.activation(e[:, 1, r], e[:, 1, r], ACT.Gelu).then_inc(o_gelu, 1)

        @block.tensor
        def _(pe):
            pe.sem_inc(hid_used, HID_BUFS)
            pe.wait_ge(consts_in, 144)
            with pe.Fori(0, PAIRS) as p:
                works = [0]
                aggs = [0]

                def work_bank():
                    pe.wait_ge(work_moved, p * WORK + works[0] + 1)
                    works[0] += 1
                    return work[(works[0] - 1) % WORK_BUFS]

                def agg_bank():
                    pe.wait_ge(agg_moved, p * AGG + aggs[0] + 1)
                    aggs[0] += 1
                    return agg[(aggs[0] - 1) % AGG_BUFS]

                def s_rows(k):
                    b = k % 2
                    pe.wait_ge(s_ready, p * PREPS + k + 1)
                    for i in range(S_TILES):
                        bank = work_bank()
                        for t in range(UR):
                            col = sj[:, b, i * UR + t:i * UR + t + 1]
                            ins = pe.transpose(bank[:, t * P:(t + 1) * P], col.to_broadcast([P, P]), ident[:])
                        ins.then_inc(work_done, 1)

                def broadcast(g):
                    l, b, half = unit(g)
                    pe.wait_ge(cols_ready, p * PREPS + l * 2 + b + 1)
                    if g >= 1:
                        pe.wait_ge(exps_done, p * PT + g * NT)
                    for bank, col in ((g_bc, G), (h_bc, H)):
                        for t in range(UR):
                            c = half * UR + t
                            ins = pe.transpose(bank[:, t * P:(t + 1) * P], col[:, b, c:c + 1].to_broadcast([P, P]), ident[:])
                    ins.then_inc(bcast_done, 1)

                def aggregate(g):
                    l, b, half = unit(g)
                    for r in range(UR):
                        bank = agg_bank()
                        for t in range(NT):
                            if r == 0:
                                pe.wait_ge(prob_ready, p * PT + g * NT + t + 1)
                            ins = pe.matmul(bank[:, 0:D + 1], prob[:, g % 2, t, r * P:(r + 1) * P], X[b][:, t, :],
                                            start=(t == 0), stop=(t == NT - 1))
                        ins.then_inc(agg_done, 1)

                def turn(src, ready):
                    for d in range(KD):
                        bank = work_bank()
                        for r in range(UR):
                            if d == 0:
                                ready(r)
                            ins = pe.transpose(bank[:, r * P:(r + 1) * P], src[:, r, d * P:(d + 1) * P], ident[:])
                        ins.then_inc(work_done, 1)

                def feed_forward(u, slot, hin, second, between):
                    base = [0] * KH

                    def first(k):
                        bank = work_bank()
                        base[k] = works[0]
                        for d in range(KD):
                            ins = pe.matmul(bank[:, 0:U], w1s[:, slot, d, k * P:(k + 1) * P], hin[:, d], start=(d == 0), stop=(d == KD - 1))
                        ins.then_inc(work_done, 1)

                    def other(k):
                        if k == 0:
                            pe.wait_ge(ff_moved, p * UNITS + u + 1)
                        pe.wait_ge(work_moved, p * WORK + base[k] + WORK_BUFS)
                        second(k).then_inc(hid_used, 1)

                    first(0)
                    for k in range(1, KH):
                        first(k)
                        between(k - 1)
                        other(k - 1)
                    between(KH - 1)
                    other(KH - 1)

                s_rows(0)
                s_rows(1)
                broadcast(0)
                for g in range(GNN):
                    l, b, half = unit(g)
                    if g + 1 < GNN:
                        broadcast(g + 1)
                    aggregate(g)
                    turn(h, lambda r: pe.wait_ge(h_ready, p * GNN * UR + g * UR + r + 1))
                    if g % (2 * HALVES) == 0:
                        pe.wait_ge(w_loaded[l], p * 32 + 32)
                    pe.wait_ge(work_moved, p * WORK + works[0] + WORK_BUFS)

                    def second(k):
                        for r in range(UR):
                            ins = pe.matmul(ff[r // 2][:, r % 2 * D:(r % 2 + 1) * D], hid[:, k % HID_BUFS, r * P:(r + 1) * P],
                                            w2s[:, l % W_SLOTS, k], start=(k == 0 and r % 2 == 0), stop=(k == KH - 1),
                                            skip_group_check=True)
                        return ins

                    def between(k):
                        if k == S_AT and prep_after(g) is not None:
                            s_rows(prep_after(g))

                    feed_forward(g, l % W_SLOTS, hT, second, between)

                def front(f):
                    turn(h, lambda r: pe.wait_ge(front_ready, p * FFN + f + 1))
                    turn(e[:, 0], lambda r: None)

                front(0)
                for f in range(FFN):
                    stage = L + f // 2
                    if f % 2 == 0:
                        pe.wait_ge(w_loaded[stage], p * 48 + 48)
                    pe.wait_ge(work_moved, p * WORK + works[0] + WORK_BUFS)
                    for d in range(KD):
                        bank = agg_bank()
                        for c in range(KD):
                            ins = pe.matmul(bank[:, 0:U], attn_ws[:, c, d * P:(d + 1) * P], nT[:, c], start=(c == 0), stop=(c == KD - 1))
                        ins.then_inc(agg_done, 1)
                    pe.wait_ge(agg_moved, p * AGG + aggs[0] + AGG_BUFS)

                    def second(k):
                        for d in range(KD):
                            ins = pe.matmul(ff[d][:, 0:U], w2s[:, stage % W_SLOTS, k, d * P:(d + 1) * P], hid[:, k % HID_BUFS],
                                            start=(k == 0), stop=(k == KH - 1))
                        return ins

                    feed_forward(GNN + f, stage % W_SLOTS, xfT, second, lambda k: None)
                    if f + 1 < FFN:
                        front(f + 1)
                    pe.wait_ge(ff_moved, p * UNITS + GNN + f + 2)
                    for r in range(UR):
                        bank = agg_bank()
                        for c in range(KD):
                            ins = pe.matmul(bank[:, 0:D], yT[:, c, r * P:(r + 1) * P], next_ws[:, c], start=(c == 0), stop=(c == KD - 1))
                        ins.then_inc(agg_done, 1)


def kernel(**inputs):
    import numpy as np
    import concourse.bacc as bacc
    from concourse.bass_utils import run_bass_kernel_spmd

    a = {k: np.asarray(v) for k, v in inputs.items()}
    B, N, D = a["x"].shape
    L, E = a["L0_gnn_W1"].shape[0], a["L0_ffn_fc1_w"].shape[0]
    HID = a["L0_gnn_W1"].shape[2]

    def tiled(w):
        return np.moveaxis(w.reshape(*w.shape[:-2], w.shape[-2] // P, P, w.shape[-1]), -2, -3)

    def columns(v):
        return np.swapaxes(v.reshape(*v.shape[:-1], v.shape[-1] // P, P), -1, -2)

    arrays = {
        "x": tiled(a["x"]),
        "adj": a["adj"],
        "adj_t": tiled(np.swapaxes(a["adj"], 1, 2)),
        "attn_rows": a["L0_gnn_attn_w"].reshape(L, 2, D),
        "attn_b": a["L0_gnn_attn_b"],
        "w1": tiled(a["L0_gnn_W1"]),
        "b1": np.moveaxis(columns(a["L0_gnn_b1"]), 0, 1),
        "w2": tiled(a["L0_gnn_W2"]),
        "rows": np.stack([a[f"L0_gnn_{n}"] for n in ("b2", "g1", "beta1", "g2", "beta2")], 1),
        "ffn_cols": np.moveaxis(columns(np.stack([a[f"L0_ffn_{n}"] for n in ("ln_g", "ln_b", "attn_b")])), 0, 1),
        "attn_w": tiled(a["L0_ffn_attn_w"].T),
        "fc1": tiled(np.swapaxes(a["L0_ffn_fc1_w"], 1, 2)),
        "fc2": tiled(np.swapaxes(a["L0_ffn_fc2_w"], 1, 2)),
        "expert_cols": np.concatenate([columns(a["L0_ffn_fc1_b"]), columns(a["L0_ffn_fc2_b"])], 2),
        "next_w": tiled(a["L0_ffn_next_w"].T),
        "next_b": a["L0_ffn_next_b"],
        "eye": np.eye(P, dtype=np.float32),
    }
    arrays = {k: np.ascontiguousarray(v) for k, v in arrays.items()}
    nc = bacc.Bacc("TRN2", target_bir_lowering=False, num_devices=1)
    args = [nc.dram_tensor(f"in_{k}", v.shape, mybir.dt.from_np(v.dtype), kind="ExternalInput").ap() for k, v in arrays.items()]
    out = nc.dram_tensor("out", arrays["x"].shape, F32, kind="ExternalOutput").ap()
    adj_ffn_kernel(nc, *args, out)
    r = run_bass_kernel_spmd(nc, [{f"in_{k}": v for k, v in arrays.items()}], core_ids=[0])
    return np.moveaxis(r.results[0]["out"], 1, 2).reshape(B, N, D)
```

```python
from contextlib import ExitStack

import concourse.bass as bass
from concourse import mybir

P = 128
F32 = mybir.dt.float32
BF16 = mybir.dt.bfloat16
I32 = mybir.dt.int32
U8 = mybir.dt.uint8
ALU = mybir.AluOpType
ACT = mybir.ActivationFunctionType
AX = mybir.AxisListType


def adj_ffn_kernel(nc, x, adj, adj_t, attn_rows, attn_b, w1, b1, w2, rows, ffn_cols, attn_w, fc1, fc2, expert_cols,
                   next_w, next_b, eye, out):
    B, _, NT, D = x.shape
    N = NT * P
    L = w1.shape[0]
    KD = D // P
    HID = w1.shape[3]
    KH = HID // P
    PAIRS = B // 2
    UR = 4
    U = UR * P
    HALVES = NT // UR
    EPS = 1e-5
    SLOPE = 0.2

    GNN = L * 2 * HALVES
    FFN = 2 * HALVES
    UNITS = GNN + FFN
    PREPS = L * 2
    S_TILES = N // U
    WORK = PREPS * S_TILES + GNN * (KD + KH) + FFN * (2 * KD + KH)
    AGG = GNN * UR + FFN * (KD + UR)
    HIDS = UNITS * KH
    PT = GNN * NT
    NORMS = 2 + GNN * (UR + 1) + FFN * 2
    WORK_BUFS, AGG_BUFS, HID_BUFS = 2, 2, 4
    W_SLOTS = 3
    STAGES = L + HALVES
    TAIL = 3
    S_AT = 4
    P_PLAN = ((1, 2, 3, 4, 6, 8), (0, 0, 1, 2, 5, 8))
    B_AT = (0, 2)
    O_AT = 2

    def unit(g):
        g = g % GNN
        return g // (2 * HALVES), g // HALVES % 2, g % HALVES

    def prep_after(g):
        l, b, half = unit(g)
        if half == 0 and b == 1 and l + 1 < L:
            return 2 * (l + 1)
        if half == 0 and b == 0:
            return 2 * l + 1
        return None

    s_tile_end, hT_end, front_end, last_tile = {0: S_TILES}, {}, {}, {}
    tiles = S_TILES
    for g in range(GNN):
        hT_end[g] = tiles + KD
        if prep_after(g) is not None:
            s_tile_end[prep_after(g)] = tiles + KD + S_AT + 2 + S_TILES
            tiles += S_TILES
        tiles += KD + KH
    for f in range(FFN):
        tiles += 2 * KD
        front_end[f] = tiles
        if f == FFN - 1:
            s_tile_end[PREPS] = tiles + O_AT + 2 + S_TILES
            tiles += S_TILES
        tiles += KH
        last_tile[f] = GNN * UR + (f + 2) * KD + f * UR - (KD if f == FFN - 1 else 0)
    assert tiles == WORK + S_TILES

    with ExitStack() as ctx:
        def sb(name, shape, dt=F32):
            return ctx.enter_context(nc.sbuf_tensor(name, shape, dt))

        def sem(name):
            return ctx.enter_context(nc.semaphore(name))

        X = [sb(f"X{i}", [P, NT, D + 1]) for i in range(2)]
        mask = [sb(f"mask{i}", [P, NT, N], U8) for i in range(2)]
        nbr = [sb(f"nbr{i}", [P, NT, N], U8) for i in range(2)]
        prob = sb("prob", [P, 2, NT, U])
        branch = sb("branch", [P, NT, U])
        hid = sb("hid", [P, HID_BUFS, U])
        w1s = sb("w1s", [P, W_SLOTS, KD, HID])
        w2s = sb("w2s", [P, W_SLOTS, KH, D])
        h = sb("h", [P, UR, D])
        e = sb("e", [P, 2, UR, D])
        hT = sb("hT", [P, KD, U])
        s_row = sb("s_row", [P, N])
        junk = sb("junk", [P, 2, N], BF16)
        row_s = sb("row_s", [P, L, 5, D])
        attn_row = sb("attn_row", [P, L, 2, D])
        attn_bias = sb("attn_bias", [P, L])
        b1s = sb("b1s", [P, L, KH])
        ffn_col = sb("ffn_col", [P, 3, KD])
        exp_col = sb("exp_col", [P, HALVES, KH + KD])
        attn_ws = sb("attn_ws", [P, KD, D])
        next_ws = sb("next_ws", [P, KD, D])
        next_row = sb("next_row", [P, D])
        ident = sb("ident", [P, P])
        ident8 = sb("ident8", [P, P], U8)
        si = sb("si", [P, 2, NT])
        sj = sb("sj", [P, 2, NT])
        sj2 = sb("sj2", [P, 2, NT])
        G = sb("G", [P, 2, NT])
        H = sb("H", [P, 2, NT])
        c_col = sb("c_col", [P, NT])
        m_col = sb("m_col", [P, NT])
        u_col = sb("u_col", [P, NT])
        smin = sb("smin", [P, 1])
        rden = sb("rden", [P, UR, 1])
        stats = sb("stats", [P, NT, 6])
        mv = sb("mv", [P, NT, 2])
        var_e = sb("var_e", [P, NT])
        rstd = sb("rstd", [P, NT])
        neg_half = sb("neg_half", [P, NT])
        eps_row = sb("eps_row", [P, NT])

        xfT = prob[:, 1, 0:KD, :]
        nT = prob[:, 1, KD:2 * KD, :]
        yT = prob[:, 1, 2 * KD:3 * KD, :]
        x_in = branch[:, :, :].rearrange("p (f a) (b d) -> p f (a b) d", f=FFN, d=D)

        agg = [ctx.enter_context(nc.psum_tensor(f"agg{i}", [P, 512], F32)) for i in range(2)]
        ff = [ctx.enter_context(nc.psum_tensor(f"ff{i}", [P, 512], F32)) for i in range(2)]
        work = [ctx.enter_context(nc.psum_tensor(f"work{i}", [P, 512], F32)) for i in range(2)]
        g_bc = ctx.enter_context(nc.psum_tensor("g_bc", [P, 512], F32))
        h_bc = ctx.enter_context(nc.psum_tensor("h_bc", [P, 512], F32))

        consts_in = sem("consts_in")
        ident8_in = sem("ident8_in")
        x_loaded = [sem(f"x_loaded{b}") for b in range(2)]
        xin_loaded = sem("xin_loaded")
        mask_loaded = [sem(f"mask_loaded{b}") for b in range(2)]
        w_loaded = [sem(f"w_loaded{i}") for i in range(STAGES)]
        x1_stored = [sem(f"x1_stored{f}") for f in range(FFN)]
        stored = sem("stored")
        work_done = sem("work_done")
        work_moved = sem("work_moved")
        agg_done = sem("agg_done")
        agg_moved = sem("agg_moved")
        hid_used = sem("hid_used")
        ff_moved = sem("ff_moved")
        bcast_done = sem("bcast_done")
        exps_done = sem("exps_done")
        prob_ready = sem("prob_ready")
        s_ready = sem("s_ready")
        cols_ready = sem("cols_ready")
        h_ready = sem("h_ready")
        var_ready = sem("var_ready")
        rstd_ready = sem("rstd_ready")
        hb_ready = sem("hb_ready")
        z_ready = sem("z_ready")
        x_ready = sem("x_ready")
        x1_ready = sem("x1_ready")
        front_ready = sem("front_ready")
        o_gelu = sem("o_gelu")
        dve_step = sem("dve_step")
        pool_step = sem("pool_step")
        norm_consts = sem("norm_consts")
        ones_set = sem("ones_set")

        block = ctx.enter_context(nc.Block())

        def x_rows(tensor, q, b, a, n):
            return tensor[bass.ds(q + b * PAIRS, 1), :, a:a + n, :].rearrange("o p t d -> p (o t) d")

        @block.sync
        def _(sp):
            def load_x(q, b):
                sp.dma_start(X[b][:, :, 0:D], x_rows(x, q, b, 0, NT)).then_inc(x_loaded[b], 16)

            def load_w(s, p=0):
                slot = slice(s % W_SLOTS, s % W_SLOTS + 1)
                if s < L:
                    sp.dma_start(w1s[:, slot], w1[s:s + 1].rearrange("e p k n -> p e k n")).then_inc(w_loaded[s], 16)
                    sp.dma_start(w2s[:, slot], w2[s:s + 1].rearrange("e p k n -> p e k n")).then_inc(w_loaded[s], 16)
                else:
                    j = p * HALVES + (s - L)
                    sp.dma_start(w1s[:, slot], fc1[bass.ds(j, 1)].rearrange("e p k n -> p e k n")).then_inc(w_loaded[s], 16)
                    sp.dma_start(w2s[:, slot], fc2[bass.ds(j, 1)].rearrange("e p k n -> p e k n")).then_inc(w_loaded[s], 16)
                    sp.dma_start(exp_col[:, s - L:s - L + 1], expert_cols[bass.ds(j, 1)].rearrange("e p n -> p e n"))\
                        .then_inc(w_loaded[s], 16)

            def pair(p, last):
                sp.wait_ge(hid_used, p * HIDS + HID_BUFS)
                load_w(1)
                for s in range(L, STAGES):
                    sp.wait_ge(hid_used, p * HIDS + (s - L + 1) * 2 * HALVES * KH + HID_BUFS)
                    load_w(s, p)
                sp.wait_ge(prob_ready, p * PT + PT)
                for f in range(FFN):
                    sp.dma_start(x_in[:, f], x_rows(x, p, f % 2, f // 2 * UR, UR)).then_inc(xin_loaded, 16)
                for f in range(FFN):
                    b, half = f % 2, f // 2
                    sp.wait_ge(x1_ready, p * FFN + f + 1)
                    sp.dma_start(x_rows(out, p, b, half * UR, UR), X[b][:, half * UR:(half + 1) * UR, 0:D])\
                        .then_inc(x1_stored[f], 16)
                    if half == HALVES - 1 and not last:
                        for i in range(b, FFN, 2):
                            sp.wait_ge(x1_stored[i], p * 16 + 16)
                        sp.wait_ge(front_ready, p * FFN + f + 1)
                        load_x(p + 1, b)
                if not last:
                    sp.wait_ge(hid_used, p * HIDS + GNN * KH + HID_BUFS)
                    load_w(2)
                    sp.wait_ge(hid_used, p * HIDS + (GNN + 2) * KH + HID_BUFS)
                    load_w(0)

            load_x(0, 0)
            for dst, src in ((attn_row[:], attn_rows.partition_broadcast(P)), (ident[:], eye),
                             (attn_bias[:], attn_b.partition_broadcast(P)), (b1s[:], b1), (ffn_col[:], ffn_cols),
                             (row_s[:], rows.partition_broadcast(P)),
                             (attn_ws[:], attn_w), (next_ws[:], next_w), (next_row[:], next_b.partition_broadcast(P))):
                sp.dma_start(dst, src).then_inc(consts_in, 16)
            load_x(0, 1)
            load_w(0)
            load_w(2)
            with sp.Fori(0, PAIRS - 1) as p:
                pair(p, False)
            pair(PAIRS - 1, True)
            for i in range(FFN):
                sp.wait_ge(x1_stored[i], PAIRS * 16)

        @block.gpsimd
        def _(pool):
            steps = [0]
            norms = [0]

            def load_masks(q):
                for b in range(2):
                    pool.dma_start(mask[b][:], adj_t[bass.ds(q + b * PAIRS, 1)].rearrange("o p t n -> p (o t) n"))\
                        .then_inc(mask_loaded[b], 16)
                    pool.dma_start(nbr[b][:], adj[bass.ds(q + b * PAIRS, 1)].rearrange("o p t n -> p (o t) n"))\
                        .then_inc(mask_loaded[b], 16)

            def step(ins):
                steps[0] += 1
                ins.then_inc(pool_step, 1)
                return steps[0]

            def power(p, a, b):
                pool.wait_ge(var_ready, p * NORMS + norms[0] + 1)
                n = step(pool.tensor_tensor(var_e[:, a:b], mv[:, a:b, 1], eps_row[:, a:b], ALU.add))
                pool.wait_ge(pool_step, n)
                pool.tensor_tensor(rstd[:, a:b], var_e[:, a:b], neg_half[:, a:b], ALU.pow).then_inc(rstd_ready, 1)
                norms[0] += 1

            def add_b2(p, g):
                for r in range(UR):
                    pool.wait_ge(h_ready, p * GNN * UR + g * UR + r + 1)
                    pool.tensor_tensor(e[:, g % 2, r], h[:, r], row_s[:, unit(g)[0], 0], ALU.add).then_inc(hb_ready, 1)

            def affine(p, g):
                l, b, half = unit(g)
                for r in range(UR):
                    pool.wait_ge(z_ready, p * GNN * UR + g * UR + r + 1)
                    n = step(pool.tensor_tensor(e[:, g % 2, r], e[:, g % 2, r], row_s[:, l, 3], ALU.mult))
                    pool.wait_ge(pool_step, n)
                    pool.tensor_tensor(X[b][:, half * UR + r, 0:D], e[:, g % 2, r], row_s[:, l, 4], ALU.add)\
                        .then_inc(x_ready, 1)

            def output(p, f):
                pool.wait_ge(x1_stored[f], p * 16 + 16)
                pool.wait_ge(o_gelu, p * FFN * UR + (f + 1) * UR)
                pool.dma_start(x_rows(out, p, f % 2, f // 2 * UR, UR), e[:, 1], accum_op=ALU.add).then_inc(stored, 16)

            def pair(p, last):
                pool.sem_clear(pool_step)
                steps[0] = 0
                norms[0] = 2
                for g in range(GNN):
                    for r in range(UR):
                        power(p, r, r + 1)
                    add_b2(p, g)
                    if g >= 1:
                        power(p, UR, 2 * UR)
                        affine(p, g - 1)
                for _ in range(2):
                    power(p, 0, UR)
                power(p, UR, 2 * UR)
                affine(p, GNN - 1)
                if not last:
                    load_masks(p + 1)
                for f in range(FFN):
                    if f >= 1:
                        output(p, f - 1)
                    if f + 1 < FFN:
                        for _ in range(2):
                            power(p, 0, UR)
                    if f >= 2 and not last:
                        power(p, 0, NT)
                output(p, FFN - 1)
                pool.wait_ge(pool_step, steps[0])
                pool.wait_ge(stored, p * FFN * 16 + FFN * 16)

            pool.memset(neg_half[:], -0.5).then_inc(norm_consts, 1)
            pool.memset(eps_row[:], EPS).then_inc(norm_consts, 1)
            pool.dma_start(ident8[:], eye).then_inc(ident8_in, 16)
            load_masks(0)
            pool.wait_ge(norm_consts, 2)
            pool.wait_ge(consts_in, 144)
            for _ in range(2):
                power(0, 0, NT)
            pool.wait_ge(pool_step, steps[0])
            with pool.Fori(0, PAIRS - 1) as p:
                pair(p, False)
            pair(PAIRS - 1, True)

        @block.vector
        def _(dve):
            steps = [0]
            norms = [0]
            aggs = [0]

            def step(ins):
                steps[0] += 1
                ins.then_inc(dve_step, 1)
                return steps[0]

            def need(n):
                dve.wait_ge(dve_step, n)

            def ask_rstd(tiles):
                ns = [step(dve.bn_stats(stats[:, t, :], src)) for t, src in tiles]
                for (t, _), n in zip(tiles, ns):
                    need(n)
                    ins = dve.bn_aggr(mv[:, t, :], stats[:, t, :])
                ins.then_inc(var_ready, 1)
                norms[0] += 1
                return norms[0]

            def normalise(dst, src, t):
                return dve.tensor_scalar(dst, src, mv[:, t, 0:1], rstd[:, t:t + 1], ALU.subtract, ALU.mult)

            def dots(l, b, t):
                for which, col in ((0, si), (1, sj)):
                    if steps[0] >= 2:
                        need(steps[0] - 1)
                    n = step(dve.tensor_tensor_reduce(junk[:, which, 0:D], X[b][:, t, 0:D], attn_row[:, l, which],
                                                      1.0, 0.0, ALU.mult, ALU.add, col[:, b, t:t + 1]))
                return n

            def start_graph(p, q, b, k):
                dve.wait_ge(x_loaded[b], q * 16 + 16)
                asked = ask_rstd([(t, X[b][:, t, 0:D]) for t in range(NT)])
                dve.wait_ge(mask_loaded[b], q * 32 + 32)
                for t in range(NT):
                    own = mask[b][:, t, t * P:(t + 1) * P]
                    step(dve.tensor_tensor(own, own, ident8[:], ALU.add))
                dve.wait_ge(rstd_ready, p * NORMS + asked)
                for t in range(NT):
                    n = step(normalise(X[b][:, t, 0:D], X[b][:, t, 0:D], t))
                need(n)
                for t in range(NT):
                    n = dots(0, b, t)
                need(n)
                dve.tensor_scalar(sj2[:, b], sj[:, b], SLOPE, None, ALU.mult).then_inc(s_ready, 1)
                dve.wait_ge(s_ready, p * PREPS + k + 1)

            def prepare(p, k):
                l, b = k % PREPS // 2, k % 2
                dve.wait_ge(work_moved, p * WORK + s_tile_end[k] + WORK_BUFS)
                need(step(dve.tensor_reduce(smin[:], s_row[:], AX.X, ALU.min)))
                need(step(dve.tensor_scalar(s_row[:], s_row[:], smin[:], 1.0, ALU.subtract, ALU.add)))
                for t in range(NT):
                    n = step(dve.tensor_tensor_reduce(junk[:, t % 2], nbr[b][:, t], s_row[:], 1.0, 0.0, ALU.mult, ALU.max,
                                                      u_col[:, t:t + 1]))
                    need(n - 1)
                need(n)
                need(step(dve.tensor_scalar(u_col[:], u_col[:], -1.0, smin[:], ALU.add, ALU.add)))
                need(step(dve.tensor_tensor(u_col[:], u_col[:], sj[:, b], ALU.max)))
                need(step(dve.tensor_scalar(c_col[:], si[:, b], attn_bias[:, l:l + 1], None, ALU.add)))
                need(step(dve.tensor_tensor(u_col[:], u_col[:], c_col[:], ALU.add)))
                need(step(dve.scalar_tensor_tensor(m_col[:], u_col[:], SLOPE, u_col[:], ALU.mult, ALU.max)))
                step(dve.tensor_tensor(G[:, b], c_col[:], m_col[:], ALU.subtract))
                dve.scalar_tensor_tensor(H[:, b], c_col[:], SLOPE, m_col[:], ALU.mult, ALU.subtract).then_inc(cols_ready, 1)

            def probabilities(p, g, t0, t1):
                l, b, half = unit(g)
                for t in range(t0, t1):
                    dve.wait_ge(exps_done, p * PT + g * NT + t + 1)
                    need(step(dve.tensor_tensor(prob[:, g % 2, t], prob[:, g % 2, t], branch[:, t], ALU.max)))
                    dve.tensor_tensor(prob[:, g % 2, t], prob[:, g % 2, t], mask[b][:, t, half * U:(half + 1) * U], ALU.min)\
                        .then_inc(prob_ready, 1)

            def first_norm(p, g, r, t0, t1):
                l, b, half = unit(g)
                bank = agg[aggs[0] % AGG_BUFS]
                dve.wait_ge(agg_done, p * AGG + aggs[0] + 1)
                if r == 0 and g >= 1:
                    dve.wait_ge(work_done, p * WORK + hT_end[g - 1])
                    dve.wait_ge(hb_ready, p * GNN * UR + g * UR)
                need(step(dve.reciprocal(rden[:, r], bank[:, D:D + 1])))
                dve.scalar_tensor_tensor(h[:, r], bank[:, 0:D], rden[:, r], X[b][:, half * UR + r, 0:D], ALU.mult, ALU.add)\
                    .then_inc(agg_moved, 1)
                aggs[0] += 1
                dve.wait_ge(agg_moved, p * AGG + aggs[0] + AGG_BUFS)
                asked = ask_rstd([(r, h[:, r])])
                probabilities(p, g + 1, t0, t1)
                dve.wait_ge(rstd_ready, p * NORMS + asked)
                need(step(normalise(h[:, r], h[:, r], r)))
                need(step(dve.tensor_tensor(h[:, r], h[:, r], row_s[:, l, 1], ALU.mult)))
                dve.tensor_tensor(h[:, r], h[:, r], row_s[:, l, 2], ALU.add).then_inc(h_ready, 1)

            def second_norm(p, g, t0, t1):
                l, b, half = unit(g)
                dve.wait_ge(hid_used, p * HIDS + (g + 1) * KH + HID_BUFS)
                dve.wait_ge(hb_ready, p * GNN * UR + (g + 1) * UR)
                for r in range(UR):
                    ins = dve.tensor_tensor(e[:, g % 2, r], ff[r // 2][:, r % 2 * D:(r % 2 + 1) * D], e[:, g % 2, r], ALU.add)
                    if r < UR - 1:
                        step(ins)
                ins.then_inc(ff_moved, 1)
                dve.wait_ge(ff_moved, p * UNITS + g + 2)
                asked = ask_rstd([(UR + r, e[:, g % 2, r]) for r in range(UR)])
                probabilities(p, g + 2, t0, t1)
                dve.wait_ge(rstd_ready, p * NORMS + asked)
                for r in range(UR):
                    normalise(e[:, g % 2, r], e[:, g % 2, r], UR + r).then_inc(z_ready, 1)

            def second_dots(p, g):
                l, b, half = unit(g)
                for r in range(UR):
                    dve.wait_ge(x_ready, p * GNN * UR + g * UR + r + 1)
                    n = dots(l + 1, b, half * UR + r)
                if half == HALVES - 1:
                    need(n)
                    dve.tensor_scalar(sj2[:, b], sj[:, b], SLOPE, None, ALU.mult).then_inc(s_ready, 1)
                    dve.wait_ge(s_ready, p * PREPS + (l + 1) * 2 + b + 1)

            def front(p, f):
                b, half = f % 2, f // 2
                a = half * UR
                dve.wait_ge(x_ready, p * GNN * UR + max(GNN - 2 * HALVES + b * HALVES + half + 1, GNN - 1) * UR)
                dve.wait_ge(xin_loaded, p * FFN * 16 + FFN * 16)
                dve.tensor_tensor(X[b][:, a:a + UR, 0:D], X[b][:, a:a + UR, 0:D], x_in[:, f], ALU.add).then_inc(x1_ready, 1)
                dve.wait_ge(x1_ready, p * FFN + f + 1)
                asked = ask_rstd([(r, X[b][:, a + r, 0:D]) for r in range(UR)])
                dve.wait_ge(rstd_ready, p * NORMS + asked)
                for r in range(UR):
                    n = step(normalise(h[:, r], X[b][:, a + r, 0:D], r))
                need(n)
                asked = ask_rstd([(r, h[:, r]) for r in range(UR)])
                dve.wait_ge(rstd_ready, p * NORMS + asked)
                for r in range(UR):
                    ins = normalise(e[:, 0, r], h[:, r], r)
                    if r < UR - 1:
                        step(ins)
                ins.then_inc(front_ready, 1)

            def attention_out(p, f):
                for d in range(KD):
                    dve.wait_ge(agg_done, p * AGG + aggs[0] + 1)
                    dve.wait_ge(work_moved, p * WORK + front_end[f] + WORK_BUFS)
                    dve.scalar_tensor_tensor(xfT[:, d], agg[aggs[0] % AGG_BUFS][:, 0:U], ffn_col[:, 2, d:d + 1], xfT[:, d],
                                             ALU.add, ALU.add).then_inc(agg_moved, 1)
                    aggs[0] += 1

            def expert_out(p, f):
                dve.wait_ge(hid_used, p * HIDS + (GNN + f + 1) * KH + HID_BUFS)
                for d in range(KD):
                    ins = dve.tensor_scalar(yT[:, d], ff[d][:, 0:U], exp_col[:, f // 2, KH + d:KH + d + 1], None, ALU.add)
                    if d < KD - 1:
                        step(ins)
                ins.then_inc(ff_moved, 1)

            def last_out(p, f):
                for r in range(UR):
                    dve.wait_ge(agg_done, p * AGG + aggs[0] + 1)
                    if r == 0 and f > 0:
                        dve.wait_ge(stored, p * FFN * 16 + f * 16)
                    dve.tensor_tensor(e[:, 1, r], agg[aggs[0] % AGG_BUFS][:, 0:D], next_row[:], ALU.add).then_inc(agg_moved, 1)
                    aggs[0] += 1

            def pair(p, last):
                dve.sem_clear(dve_step)
                steps[0], norms[0], aggs[0] = 0, 2, 0
                for g in range(GNN):
                    l, b, half = unit(g)
                    made = P_PLAN[half] if g + 1 < GNN else (0,) * (UR + 2)
                    for r in range(UR):
                        first_norm(p, g, r, made[r - 1] if r else 0, made[r])
                    if g >= 1:
                        second_norm(p, g - 1, made[UR - 1], made[UR])
                        if unit(g - 1)[0] + 1 < L:
                            second_dots(p, g - 1)
                        probabilities(p, g + 1, made[UR], made[UR + 1])
                    else:
                        probabilities(p, g + 1, made[UR - 1], made[UR + 1])
                    if prep_after(g) is not None:
                        prepare(p, prep_after(g))
                dve.wait_ge(work_done, p * WORK + hT_end[GNN - 1])
                dve.wait_ge(hb_ready, p * GNN * UR + GNN * UR)
                front(p, 0)
                for f in range(FFN):
                    attention_out(p, f)
                    if f == 0:
                        second_norm(p, GNN - 1, 0, 0)
                    else:
                        expert_out(p, f - 1)
                        last_out(p, f - 1)
                    if f + 1 < FFN:
                        front(p, f + 1)
                    if f == 2 and not last:
                        start_graph(p, p + 1, 0, PREPS)
                    if f == 3 and not last:
                        prepare(p, PREPS)
                        start_graph(p, p + 1, 1, PREPS + 1)
                expert_out(p, FFN - 1)
                last_out(p, FFN - 1)
                if not last:
                    probabilities(p, GNN, 0, NT)
                dve.wait_ge(dve_step, steps[0])

            for b in range(2):
                dve.memset(X[b][:, :, D:D + 1], 1.0).then_inc(ones_set, 1)
            dve.sem_inc(agg_moved, AGG_BUFS)
            dve.sem_inc(ff_moved, 1)
            dve.wait_ge(consts_in, 144)
            dve.wait_ge(ident8_in, 16)
            dve.wait_ge(ones_set, 2)
            start_graph(0, 0, 0, 0)
            prepare(0, 0)
            start_graph(0, 0, 1, 1)
            probabilities(0, 0, 0, NT)
            dve.wait_ge(dve_step, steps[0])
            with dve.Fori(0, PAIRS - 1) as p:
                pair(p, False)
            pair(PAIRS - 1, True)

        @block.scalar
        def _(act):
            works = [0]

            def branches(p, g):
                l, b, half = unit(g)
                act.wait_ge(bcast_done, p * GNN + g + 1)
                if g >= 2:
                    act.wait_ge(agg_done, p * AGG + (min(g, GNN) - 1) * UR)
                for t in range(NT):
                    act.activation(prob[:, g % 2, t], g_bc[:, 0:U], ACT.Exp, bias=sj[:, b, t:t + 1])
                    if g >= 1:
                        act.wait_ge(prob_ready, p * PT + (g - 1) * NT + t + 1)
                    act.activation(branch[:, t], h_bc[:, 0:U], ACT.Exp, bias=sj2[:, b, t:t + 1]).then_inc(exps_done, 1)

            def move(p, dst, **how):
                n = works[0]
                act.wait_ge(work_done, p * WORK + n + 1)
                act.activation(dst, work[n % WORK_BUFS][:, 0:U], **how).then_inc(work_moved, 1)
                works[0] += 1

            def hidden(p, u, k, bias):
                act.wait_ge(hid_used, p * HIDS + u * KH + k + 1)
                move(p, hid[:, k % HID_BUFS], func=ACT.Gelu, bias=bias)

            def s_rows(p, k):
                if k >= 1:
                    act.wait_ge(cols_ready, p * PREPS + k)
                for t in range(S_TILES):
                    move(p, s_row[:, t * U:(t + 1) * U], func=ACT.Copy)

            def front(p, f):
                for d in range(KD):
                    move(p, xfT[:, d], func=ACT.Copy)
                for d in range(KD):
                    move(p, nT[:, d], func=ACT.Identity, scale=ffn_col[:, 0, d:d + 1], bias=ffn_col[:, 1, d:d + 1])

            def output(p, f):
                for r in range(UR):
                    act.wait_ge(agg_moved, p * AGG + last_tile[f] + r + 1 + AGG_BUFS)
                    act.activation(e[:, 1, r], e[:, 1, r], ACT.Gelu).then_inc(o_gelu, 1)

            def pair(p, last):
                works[0] = S_TILES
                for g in range(GNN):
                    l, b, half = unit(g)
                    if g + 1 < GNN:
                        branches(p, g + 1)
                    for d in range(KD):
                        move(p, hT[:, d], func=ACT.Copy)
                    for k in range(KH):
                        hidden(p, g, k, b1s[:, l, k:k + 1])
                        if k == S_AT + 1 and prep_after(g) is not None:
                            s_rows(p, prep_after(g))
                    if g == GNN - 1:
                        front(p, 0)
                for f in range(FFN):
                    for k in range(KH):
                        hidden(p, GNN + f, k, exp_col[:, f // 2, k:k + 1])
                        if k == O_AT + 1 and f >= 1:
                            output(p, f - 1)
                        if k == O_AT + 1 and f == FFN - 1 and not last:
                            s_rows(p, PREPS)
                    if f + 1 < FFN:
                        front(p, f + 1)
                if not last:
                    branches(p, GNN)
                output(p, FFN - 1)

            act.sem_inc(work_moved, WORK_BUFS)
            act.wait_ge(consts_in, 144)
            s_rows(0, 0)
            branches(0, 0)
            with act.Fori(0, PAIRS - 1) as p:
                pair(p, False)
            pair(PAIRS - 1, True)

        @block.tensor
        def _(pe):
            works = [0]
            aggs = [0]
            hid_at = {}

            def work_bank(p):
                pe.wait_ge(work_moved, p * WORK + works[0] + 1)
                works[0] += 1
                return work[(works[0] - 1) % WORK_BUFS]

            def agg_bank(p):
                pe.wait_ge(agg_moved, p * AGG + aggs[0] + 1)
                aggs[0] += 1
                return agg[(aggs[0] - 1) % AGG_BUFS]

            def s_rows(p, k):
                b = k % 2
                pe.wait_ge(s_ready, p * PREPS + k + 1)
                for i in range(S_TILES):
                    bank = work_bank(p)
                    for t in range(UR):
                        col = sj[:, b, i * UR + t:i * UR + t + 1]
                        ins = pe.transpose(bank[:, t * P:(t + 1) * P], col.to_broadcast([P, P]), ident[:])
                    ins.then_inc(work_done, 1)

            def broadcast(p, g):
                l, b, half = unit(g)
                pe.wait_ge(cols_ready, p * PREPS + g // (2 * HALVES) * 2 + b + 1)
                if g >= 1:
                    pe.wait_ge(exps_done, p * PT + g * NT)
                for bank, col in ((g_bc, G), (h_bc, H)):
                    for t in range(UR):
                        c = half * UR + t
                        ins = pe.transpose(bank[:, t * P:(t + 1) * P], col[:, b, c:c + 1].to_broadcast([P, P]), ident[:])
                ins.then_inc(bcast_done, 1)

            def aggregate(p, g):
                l, b, half = unit(g)
                for r in range(UR):
                    if r == B_AT[half] and g + 1 < GNN:
                        broadcast(p, g + 1)
                    bank = agg_bank(p)
                    for t in range(NT):
                        if r == 0:
                            pe.wait_ge(prob_ready, p * PT + g * NT + t + 1)
                        ins = pe.matmul(bank[:, 0:D + 1], prob[:, g % 2, t, r * P:(r + 1) * P], X[b][:, t, :],
                                        start=(t == 0), stop=(t == NT - 1))
                    ins.then_inc(agg_done, 1)

            def turn(p, src):
                for d in range(KD):
                    bank = work_bank(p)
                    for r in range(UR):
                        ins = pe.transpose(bank[:, r * P:(r + 1) * P], src[:, r, d * P:(d + 1) * P], ident[:])
                    ins.then_inc(work_done, 1)

            def turn_h(p, g):
                for d in range(KD):
                    bank = work_bank(p)
                    for r in range(UR):
                        if d == 0:
                            pe.wait_ge(h_ready, p * GNN * UR + g * UR + r + 1)
                        ins = pe.transpose(bank[:, r * P:(r + 1) * P], h[:, r, d * P:(d + 1) * P], ident[:])
                    ins.then_inc(work_done, 1)

            def front(p, f):
                pe.wait_ge(front_ready, p * FFN + f + 1)
                turn(p, h)
                turn(p, e[:, 0])

            def hidden(p, slot, k, hin):
                bank = work_bank(p)
                hid_at[k] = works[0]
                for d in range(KD):
                    ins = pe.matmul(bank[:, 0:U], w1s[:, slot, d, k * P:(k + 1) * P], hin[:, d], start=(d == 0), stop=(d == KD - 1))
                ins.then_inc(work_done, 1)

            def sums(p, u, k):
                if k == 0:
                    pe.wait_ge(ff_moved, p * UNITS + u + 1)
                pe.wait_ge(work_moved, p * WORK + hid_at[k] + WORK_BUFS)
                if u < GNN:
                    slot = unit(u)[0] % W_SLOTS
                    for r in range(UR):
                        ins = pe.matmul(ff[r // 2][:, r % 2 * D:(r % 2 + 1) * D], hid[:, k % HID_BUFS, r * P:(r + 1) * P],
                                        w2s[:, slot, k], start=(k == 0 and r % 2 == 0), stop=(k == KH - 1),
                                        skip_group_check=True)
                else:
                    slot = (L + (u - GNN) // 2) % W_SLOTS
                    for d in range(KD):
                        ins = pe.matmul(ff[d][:, 0:U], w2s[:, slot, k, d * P:(d + 1) * P], hid[:, k % HID_BUFS],
                                        start=(k == 0), stop=(k == KH - 1))
                ins.then_inc(hid_used, 1)

            def tail(p, u):
                for k in range(KH - TAIL, KH):
                    sums(p, u, k)

            def last_product(p, f):
                pe.wait_ge(ff_moved, p * UNITS + GNN + f + 2)
                for r in range(UR):
                    bank = agg_bank(p)
                    for c in range(KD):
                        ins = pe.matmul(bank[:, 0:D], yT[:, c, r * P:(r + 1) * P], next_ws[:, c], start=(c == 0), stop=(c == KD - 1))
                    ins.then_inc(agg_done, 1)

            def pair(p, last):
                works[0], aggs[0] = S_TILES, 0
                for g in range(GNN):
                    l, b, half = unit(g)
                    aggregate(p, g)
                    if g >= 1:
                        tail(p, g - 1)
                    turn_h(p, g)
                    if g % (2 * HALVES) == 0:
                        pe.wait_ge(w_loaded[l], p * 32 + 32)
                    pe.wait_ge(work_moved, p * WORK + works[0] + WORK_BUFS)
                    hidden(p, l % W_SLOTS, 0, hT)
                    for k in range(1, KH):
                        hidden(p, l % W_SLOTS, k, hT)
                        if k == S_AT + 1 and prep_after(g) is not None:
                            s_rows(p, prep_after(g))
                        if k <= KH - TAIL:
                            sums(p, g, k - 1)
                    if g == GNN - 1:
                        front(p, 0)
                for f in range(FFN):
                    stage = L + f // 2
                    if f % 2 == 0:
                        pe.wait_ge(w_loaded[stage], p * 48 + 48)
                    pe.wait_ge(work_moved, p * WORK + works[0] + WORK_BUFS)
                    for d in range(KD):
                        bank = agg_bank(p)
                        for c in range(KD):
                            ins = pe.matmul(bank[:, 0:U], attn_ws[:, c, d * P:(d + 1) * P], nT[:, c], start=(c == 0), stop=(c == KD - 1))
                        ins.then_inc(agg_done, 1)
                    tail(p, GNN + f - 1)
                    pe.wait_ge(agg_moved, p * AGG + aggs[0] + AGG_BUFS)
                    hidden(p, stage % W_SLOTS, 0, xfT)
                    for k in range(1, KH):
                        hidden(p, stage % W_SLOTS, k, xfT)
                        if k == O_AT + 1 and f >= 1:
                            last_product(p, f - 1)
                        if k == O_AT + 1 and f == FFN - 1 and not last:
                            s_rows(p, PREPS)
                        if k <= KH - TAIL:
                            sums(p, GNN + f, k - 1)
                    if f + 1 < FFN:
                        front(p, f + 1)
                tail(p, UNITS - 1)
                if not last:
                    broadcast(p, GNN)
                last_product(p, FFN - 1)

            pe.sem_inc(hid_used, HID_BUFS)
            pe.wait_ge(consts_in, 144)
            s_rows(0, 0)
            broadcast(0, 0)
            with pe.Fori(0, PAIRS - 1) as p:
                pair(p, False)
            pair(PAIRS - 1, True)


def kernel(**inputs):
    import numpy as np
    import concourse.bacc as bacc
    from concourse.bass_utils import run_bass_kernel_spmd

    a = {k: np.asarray(v) for k, v in inputs.items()}
    B, N, D = a["x"].shape
    L, E = a["L0_gnn_W1"].shape[0], a["L0_ffn_fc1_w"].shape[0]
    HID = a["L0_gnn_W1"].shape[2]

    def tiled(w):
        return np.moveaxis(w.reshape(*w.shape[:-2], w.shape[-2] // P, P, w.shape[-1]), -2, -3)

    def columns(v):
        return np.swapaxes(v.reshape(*v.shape[:-1], v.shape[-1] // P, P), -1, -2)

    arrays = {
        "x": tiled(a["x"]),
        "adj": tiled(a["adj"]),
        "adj_t": tiled(np.swapaxes(a["adj"], 1, 2)),
        "attn_rows": a["L0_gnn_attn_w"].reshape(L, 2, D),
        "attn_b": a["L0_gnn_attn_b"],
        "w1": tiled(a["L0_gnn_W1"]),
        "b1": np.moveaxis(columns(a["L0_gnn_b1"]), 0, 1),
        "w2": tiled(a["L0_gnn_W2"]),
        "rows": np.stack([a[f"L0_gnn_{n}"] for n in ("b2", "g1", "beta1", "g2", "beta2")], 1),
        "ffn_cols": np.moveaxis(columns(np.stack([a[f"L0_ffn_{n}"] for n in ("ln_g", "ln_b", "attn_b")])), 0, 1),
        "attn_w": tiled(a["L0_ffn_attn_w"].T),
        "fc1": tiled(np.swapaxes(a["L0_ffn_fc1_w"], 1, 2)),
        "fc2": tiled(np.swapaxes(a["L0_ffn_fc2_w"], 1, 2)),
        "expert_cols": np.concatenate([columns(a["L0_ffn_fc1_b"]), columns(a["L0_ffn_fc2_b"])], 2),
        "next_w": tiled(a["L0_ffn_next_w"].T),
        "next_b": a["L0_ffn_next_b"],
        "eye": np.eye(P, dtype=np.float32),
    }
    arrays = {k: np.ascontiguousarray(v) for k, v in arrays.items()}
    nc = bacc.Bacc("TRN2", target_bir_lowering=False, num_devices=1)
    args = [nc.dram_tensor(f"in_{k}", v.shape, mybir.dt.from_np(v.dtype), kind="ExternalInput").ap() for k, v in arrays.items()]
    out = nc.dram_tensor("out", arrays["x"].shape, F32, kind="ExternalOutput").ap()
    adj_ffn_kernel(nc, *args, out)
    r = run_bass_kernel_spmd(nc, [{f"in_{k}": v for k, v in arrays.items()}], core_ids=[0])
    return np.moveaxis(r.results[0]["out"], 1, 2).reshape(B, N, D)
```

```python
from contextlib import ExitStack

import concourse.bass as bass
from concourse import mybir

P = 128
F32 = mybir.dt.float32
F16 = mybir.dt.float16
I32 = mybir.dt.int32
U8 = mybir.dt.uint8
ALU = mybir.AluOpType
ACT = mybir.ActivationFunctionType
AX = mybir.AxisListType


def adj_ffn_kernel(nc, x, adj, adj_t, attn_rows, attn_b, w1, b1, w2, b2_rows, rows, norm_cols, ffn_cols,
                   attn_w, fc1, fc2, expert_cols, next_w, next_b, eye, out):
    B, _, NT, D = x.shape
    N = NT * P
    L = w1.shape[0]
    KD = D // P
    HID = w1.shape[3]
    KH = HID // P
    PAIRS = B // 2
    UR = 4
    U = UR * P
    HALVES = NT // UR
    EPS = 1e-5
    SLOPE = 0.2

    GNN = L * 2 * HALVES
    FFN = 2 * HALVES
    UNITS = GNN + FFN
    PREPS = L * 2
    S_TILES = N // U
    WORK = PREPS * S_TILES + GNN * KH + FFN * (2 * KD + KH)
    AGG = GNN * UR + FFN * (KD + UR)
    HIDS = UNITS * KH
    PT = GNN * NT
    NORMS = 2 + GNN * (UR + 1) + FFN * 2
    WORK_BUFS, AGG_BUFS, HID_BUFS = 2, 2, 4
    W_SLOTS = 3
    STAGES = L + HALVES
    CHUNK = 512
    CHUNKS = 2 * KD * HID // CHUNK
    TABLES = 2 * GNN
    BY_DVE = 4
    LAG = 3
    W_SCALE, IN_SCALE = 2.0 ** 8, 2.0 ** 4
    TAIL = 3
    S_AT = 4
    P_PLAN = ((1, 2, 3, 4, 5, 8), (0, 0, 1, 2, 4, 8))
    B_AT = (0, 2)
    OUT_AT = KH - 2
    NEXT_AT = 3
    O_AT = 2

    def unit(g):
        g = g % GNN
        return g // (2 * HALVES), g // HALVES % 2, g % HALVES

    def prep_after(g):
        l, b, half = unit(g)
        if half == 0 and b == 1 and l + 1 < L:
            return 2 * (l + 1)
        if half == 0 and b == 0:
            return 2 * l + 1
        return None

    FIRST_CHUNKS, PAIR_CHUNKS = CHUNKS, STAGES * CHUNKS

    s_tile_end, front_end, last_tile = {0: S_TILES}, {}, {}
    tiles = S_TILES
    for g in range(GNN):
        if prep_after(g) is not None:
            s_tile_end[prep_after(g)] = tiles + S_AT + 2 + S_TILES
            tiles += S_TILES
        tiles += KH
    for f in range(FFN):
        tiles += 2 * KD
        front_end[f] = tiles - 1
        if f == FFN - 1:
            s_tile_end[PREPS] = tiles + NEXT_AT + 2 + S_TILES
            tiles += S_TILES
        tiles += KH
        last_tile[f] = GNN * UR + (f + 2) * KD + f * UR - (KD if f == FFN - 1 else 0)
    assert tiles == WORK + S_TILES

    with ExitStack() as ctx:
        def sb(name, shape, dt=F32):
            return ctx.enter_context(nc.sbuf_tensor(name, shape, dt))

        def sem(name):
            return ctx.enter_context(nc.semaphore(name))

        X = [sb(f"X{i}", [P, NT, D + 1]) for i in range(2)]
        mask = [sb(f"mask{i}", [P, NT, N], U8) for i in range(2)]
        nbr = [sb(f"nbr{i}", [P, NT, N], U8) for i in range(2)]
        prob = sb("prob", [P, 2, NT, U])
        branch = sb("branch", [P, NT, U])
        hid = sb("hid", [P, HID_BUFS, 2, U], F16)
        w1s = sb("w1s", [P, W_SLOTS, 2, KD, HID], F16)
        w2s = sb("w2s", [P, W_SLOTS, 2, KH, D], F16)
        inT = sb("inT", [P, 2, KD, U], F16)
        hid32 = sb("hid32", [P, 2, U])
        chunk = sb("chunk", [P, 2, CHUNK])
        h = sb("h", [P, UR, D])
        e = sb("e", [P, 2, UR, D])
        s_row = sb("s_row", [P, N])
        junk = sb("junk", [P, 2, N], U8)
        row_s = sb("row_s", [P, L, 4, D])
        norm_col = sb("norm_col", [P, L, 2, KD])
        attn_row = sb("attn_row", [P, L, 2, D])
        attn_bias = sb("attn_bias", [P, L])
        b1s = sb("b1s", [P, L, KH])
        ffn_col = sb("ffn_col", [P, 3, KD])
        exp_col = sb("exp_col", [P, HALVES, KH + KD])
        attn_ws = sb("attn_ws", [P, KD, D])
        next_ws = sb("next_ws", [P, KD, D])
        next_row = sb("next_row", [P, D])
        ident = sb("ident", [P, P])
        ident8 = sb("ident8", [P, P], U8)
        si = sb("si", [P, 2, NT])
        sj = sb("sj", [P, 2, NT])
        sj2 = sb("sj2", [P, 2, NT])
        G = sb("G", [P, 2, NT])
        H = sb("H", [P, 2, NT])
        c_col = sb("c_col", [P, NT])
        m_col = sb("m_col", [P, NT])
        u_col = sb("u_col", [P, NT])
        smin = sb("smin", [P, 1])
        rden = sb("rden", [P, UR, 1])
        stats = sb("stats", [P, NT, 6])
        mv = sb("mv", [P, NT, 2])
        var_e = sb("var_e", [P, NT])
        rstd = sb("rstd", [P, NT])
        neg_half = sb("neg_half", [P, NT])
        eps_row = sb("eps_row", [P, NT])
        tick = sb("tick", [P, 1])
        act_tick = sb("act_tick", [P, 1])

        hT32 = s_row[:, :].rearrange("p (d u) -> p d u", d=KD)
        first_rows = s_row[:, :].rearrange("p (r d) -> p r d", r=UR)
        xfT = prob[:, 1, 0:KD, :]
        nT = prob[:, 1, KD:2 * KD, :]
        yT = prob[:, 1, 2 * KD:3 * KD, :]
        x_in = branch[:, :, :].rearrange("p (f a) (b d) -> p f (a b) d", f=FFN, d=D)

        agg = [ctx.enter_context(nc.psum_tensor(f"agg{i}", [P, 512], F32)) for i in range(2)]
        ff = [ctx.enter_context(nc.psum_tensor(f"ff{i}", [P, 512], F32)) for i in range(2)]
        work = [ctx.enter_context(nc.psum_tensor(f"work{i}", [P, 512], F32)) for i in range(2)]
        g_bc = ctx.enter_context(nc.psum_tensor("g_bc", [P, 512], F32))
        h_bc = ctx.enter_context(nc.psum_tensor("h_bc", [P, 512], F32))

        attn_in = sem("attn_in")
        consts_in = sem("consts_in")
        ident8_in = sem("ident8_in")
        x_loaded = [sem(f"x_loaded{b}") for b in range(2)]
        xin_loaded = sem("xin_loaded")
        mask_loaded = [sem(f"mask_loaded{b}") for b in range(2)]
        exp_in = [sem(f"exp_in{i}") for i in range(HALVES)]
        chunk_in = [sem(f"chunk_in{i}") for i in range(2)]
        b2_in = sem("b2_in")
        x1_stored = [sem(f"x1_stored{f}") for f in range(FFN)]
        stored = sem("stored")
        work_done = sem("work_done")
        work_moved = sem("work_moved")
        w_split = sem("w_split")
        turn_done = sem("turn_done")
        hT_high = sem("hT_high")
        hT_full = sem("hT_full")
        hT_low = [sem(f"hT_low{d}") for d in range(KD)]
        xaT_split = sem("xaT_split")
        hid_high = sem("hid_high")
        hid_low = [sem(f"hid_low{i}") for i in range(2)]
        table_loaded = sem("table_loaded")
        agg_done = sem("agg_done")
        agg_moved = sem("agg_moved")
        hid_used = sem("hid_used")
        ff_moved = sem("ff_moved")
        bcast_done = sem("bcast_done")
        exps_done = sem("exps_done")
        prob_ready = sem("prob_ready")
        s_ready = sem("s_ready")
        cols_ready = sem("cols_ready")
        h_ready = sem("h_ready")
        var_ready = sem("var_ready")
        rstd_ready = sem("rstd_ready")
        hb_ready = sem("hb_ready")
        z_ready = sem("z_ready")
        x_ready = sem("x_ready")
        x1_ready = sem("x1_ready")
        front_ready = sem("front_ready")
        o_gelu = sem("o_gelu")
        dve_step = sem("dve_step")
        pool_step = sem("pool_step")
        norm_consts = sem("norm_consts")
        ones_set = sem("ones_set")

        block = ctx.enter_context(nc.Block())

        def wait_low(engine, p, u, k):
            u, k = u + k // KH, k % KH
            if k < BY_DVE:
                engine.wait_ge(hid_low[0], p * UNITS * BY_DVE + u * BY_DVE + k + 1)
            else:
                engine.wait_ge(hid_low[1], p * UNITS * (KH - BY_DVE) + u * (KH - BY_DVE) + k - BY_DVE + 1)

        def x_rows(tensor, q, b, a, n):
            return tensor[bass.ds(q + b * PAIRS, 1), :, a:a + n, :].rearrange("o p t d -> p (o t) d")

        @block.sync
        def _(sp):
            def load_x(q, b):
                sp.dma_start(X[b][:, :, 0:D], x_rows(x, q, b, 0, NT)).then_inc(x_loaded[b], 16)

            def load_chunks(s, n0, a, b, p=0):
                for c in range(a, b):
                    if not (isinstance(n0, int) and n0 + c < 2):
                        sp.wait_ge(w_split, n0 + c - 1)
                    half, i = divmod(c, CHUNKS // 2)
                    if s < L:
                        src = (w1, w2)[half][s:s + 1]
                    else:
                        src = (fc1, fc2)[half][bass.ds(p * HALVES + (s - L), 1)]
                    sp.dma_start(chunk[:, c % 2], src.rearrange("e p k n -> p (e k n)")[:, i * CHUNK:(i + 1) * CHUNK])\
                        .then_inc(chunk_in[c % 2], 16)

            def store(p, f, last):
                b, half = f % 2, f // 2
                sp.wait_ge(x1_ready, p * FFN + f + 1)
                sp.dma_start(x_rows(out, p, b, half * UR, UR), X[b][:, half * UR:(half + 1) * UR, 0:D])\
                    .then_inc(x1_stored[f], 16)
                if half == HALVES - 1 and not last:
                    for i in range(b, FFN, 2):
                        sp.wait_ge(x1_stored[i], p * 16 + 16)
                    sp.wait_ge(front_ready, p * FFN + f + 1)
                    load_x(p + 1, b)

            def pair(p, last):
                n = p * PAIR_CHUNKS + FIRST_CHUNKS
                for s in range(1, L):
                    load_chunks(s, n + (s - 1) * CHUNKS, 0, CHUNKS)
                for s in range(L, STAGES):
                    sp.wait_ge(hid_used, p * HIDS + (s - L + 1) * 2 * HALVES * KH + HID_BUFS)
                    j = p * HALVES + (s - L)
                    sp.dma_start(exp_col[:, s - L:s - L + 1], expert_cols[bass.ds(j, 1)].rearrange("e p n -> p e n"))\
                        .then_inc(exp_in[s - L], 16)
                    load_chunks(s, n + (s - 1) * CHUNKS, 0, CHUNKS, p)
                n += (STAGES - 1) * CHUNKS
                if not last:
                    load_chunks(0, n, 0, 2)
                sp.wait_ge(prob_ready, p * PT + PT)
                for f in range(FFN):
                    sp.dma_start(x_in[:, f], x_rows(x, p, f % 2, f // 2 * UR, UR)).then_inc(xin_loaded, 16)
                for f in range(FFN):
                    store(p, f, last)
                if not last:
                    load_chunks(0, n, 2, CHUNKS)

            load_x(0, 0)
            for dst, src in ((attn_row[:], attn_rows.partition_broadcast(P)), (ident[:], eye),
                             (attn_bias[:], attn_b.partition_broadcast(P))):
                sp.dma_start(dst, src).then_inc(attn_in, 16)
            for dst, src in ((b1s[:], b1), (ffn_col[:], ffn_cols),
                             (norm_col[:], norm_cols),
                             (row_s[:], rows.partition_broadcast(P)),
                             (attn_ws[:], attn_w), (next_ws[:], next_w), (next_row[:], next_b.partition_broadcast(P))):
                sp.dma_start(dst, src).then_inc(consts_in, 16)
            sp.dma_start(e[:, 0, 0:L], b2_rows.partition_broadcast(P)).then_inc(b2_in, 16)
            load_x(0, 1)
            load_chunks(0, 0, 0, CHUNKS)
            with sp.Fori(0, PAIRS - 1) as p:
                pair(p, False)
            pair(PAIRS - 1, True)
            for i in range(FFN):
                sp.wait_ge(x1_stored[i], PAIRS * 16)

        @block.gpsimd
        def _(pool):
            steps = [0]
            norms = [0]

            def load_masks(q):
                for b in range(2):
                    pool.dma_start(mask[b][:], adj_t[bass.ds(q + b * PAIRS, 1)].rearrange("o p t n -> p (o t) n"))\
                        .then_inc(mask_loaded[b], 16)
                    pool.dma_start(nbr[b][:], adj[bass.ds(q + b * PAIRS, 1)].rearrange("o p t n -> p (o t) n"))\
                        .then_inc(mask_loaded[b], 16)

            def step(ins):
                steps[0] += 1
                ins.then_inc(pool_step, 1)
                return steps[0]

            def power(p, a, b):
                pool.wait_ge(var_ready, p * NORMS + norms[0] + 1)
                n = step(pool.tensor_tensor(var_e[:, a:b], mv[:, a:b, 1], eps_row[:, a:b], ALU.add))
                pool.wait_ge(pool_step, n)
                pool.tensor_tensor(rstd[:, a:b], var_e[:, a:b], neg_half[:, a:b], ALU.pow).then_inc(rstd_ready, 1)
                norms[0] += 1

            def add_b2(p, g, r):
                l = unit(g)[0]
                pool.wait_ge(h_ready, p * GNN * UR + g * UR + r + 1)
                n = step(pool.tensor_tensor(e[:, g % 2, r], h[:, r], row_s[:, l, 0], ALU.mult))
                pool.wait_ge(pool_step, n)
                pool.tensor_tensor(e[:, g % 2, r], e[:, g % 2, r], row_s[:, l, 1], ALU.add).then_inc(hb_ready, 1)

            def affine(p, g, r):
                l, b, half = unit(g)
                pool.wait_ge(z_ready, p * GNN * UR + g * UR + r + 1)
                n = step(pool.tensor_tensor(e[:, g % 2, r], e[:, g % 2, r], row_s[:, l, 2], ALU.mult))
                pool.wait_ge(pool_step, n)
                pool.tensor_tensor(X[b][:, half * UR + r, 0:D], e[:, g % 2, r], row_s[:, l, 3], ALU.add)\
                    .then_inc(x_ready, 1)

            def split_chunks(s, n0, a, b, p=None, free=None):
                if free is not None:
                    pool.wait_ge(hid_used, p * HIDS + free * KH + HID_BUFS)
                for c in range(a, b):
                    half, i = divmod(c, CHUNKS // 2)
                    dst = [(w1s, w2s)[half][:, s % W_SLOTS, j].rearrange("p k n -> p (k n)")[:, i * CHUNK:(i + 1) * CHUNK]
                           for j in range(2)]
                    pool.wait_ge(chunk_in[c % 2], (n0 + c - c % 2) * 8 + 16)
                    n = step(pool.tensor_tensor(tick[:], eps_row[:, 0:1], eps_row[:, 0:1], ALU.add))
                    pool.wait_ge(pool_step, n)
                    n = step(pool.tensor_scalar(chunk[:, c % 2], chunk[:, c % 2], W_SCALE, 1.0, ALU.mult, ALU.mult))
                    pool.wait_ge(pool_step, n)
                    n = step(pool.tensor_scalar(dst[0], chunk[:, c % 2], 1.0, 1.0, ALU.mult, ALU.mult))
                    pool.wait_ge(pool_step, n)
                    pool.tensor_tensor(dst[1], chunk[:, c % 2], dst[0], ALU.subtract).then_inc(w_split, 1)

            def hT_half(p, g):
                pool.wait_ge(hT_full, p * GNN * KD + g * KD + 1)
                pool.tensor_tensor(inT[:, 1, 0], hT32[:, 0], inT[:, 0, 0], ALU.subtract).then_inc(hT_low[0], 1)

            def hid_half(p, u, k):
                pool.wait_ge(hid_high, p * HIDS + u * KH + k + 1)
                pool.tensor_tensor(hid[:, k % HID_BUFS, 1], hid32[:, k % 2], hid[:, k % HID_BUFS, 0], ALU.subtract)\
                    .then_inc(hid_low[1], 1)

            def output(p, f):
                pool.wait_ge(x1_stored[f], p * 16 + 16)
                pool.wait_ge(o_gelu, p * FFN * UR + (f + 1) * UR)
                pool.dma_start(x_rows(out, p, f % 2, f // 2 * UR, UR), e[:, 1], accum_op=ALU.add).then_inc(stored, 16)

            def pair(p, last):
                pool.sem_clear(pool_step)
                steps[0] = 0
                norms[0] = 2
                n = p * PAIR_CHUNKS + FIRST_CHUNKS
                split = {1: 1, 3: 2, 5: 3, 9: 4}
                assert STAGES == 5
                for g in range(GNN):
                    first = 0 if g in split else CHUNKS // 2
                    s = split.get(g, split.get(g - 1))
                    here = s is not None
                    if here:
                        n0 = n + (s - 1) * CHUNKS
                        split_chunks(s, n0, first, first + 2, p, max(s - L + 1, 0) * 2 * HALVES)
                    if g == GNN - 1 and not last:
                        pool.wait_ge(prob_ready, p * PT + PT)
                        load_masks(p + 1)
                    for r in range(UR):
                        power(p, r, r + 1)
                        if here and r < 2:
                            split_chunks(s, n0, first + 2 + r, first + 3 + r)
                    hT_half(p, g)
                    if g >= 1:
                        power(p, UR, 2 * UR)
                        for r in range(UR):
                            affine(p, g - 1, r)
                    for k in range(BY_DVE, KH - UR):
                        hid_half(p, g, k)
                    if g < GNN - 1:
                        for r in range(UR):
                            add_b2(p, g, r)
                            hid_half(p, g, KH - UR + r)
                    else:
                        power(p, 0, UR)
                        for r in range(UR):
                            add_b2(p, g, r)
                            if r == 0:
                                hid_half(p, g, KH - UR)
                            if r == 1:
                                power(p, 0, UR)
                        for k in range(KH - UR + 1, KH):
                            hid_half(p, g, k)
                zero = n + (STAGES - 1) * CHUNKS
                power(p, 0, UR)
                power(p, UR, 2 * UR)
                for r in range(UR):
                    affine(p, GNN - 1, r)
                for f in range(FFN):
                    if f == 3 and not last:
                        split_chunks(0, zero, CHUNKS // 2, CHUNKS)
                    for k in range(BY_DVE, KH):
                        if (BY_DVE if f else BY_DVE + 1) <= k < BY_DVE + 2 and f < FFN - 1:
                            power(p, 0, UR)
                        if k == KH - 1 and f == 2 and not last:
                            power(p, 0, NT)
                        hid_half(p, GNN + f, k)
                        if k == OUT_AT and f >= 1:
                            output(p, f - 1)
                    if f == 2 and not last:
                        split_chunks(0, zero, 0, CHUNKS // 2, p, GNN + 2)
                if not last:
                    power(p, 0, NT)
                output(p, FFN - 1)
                pool.wait_ge(pool_step, steps[0])
                pool.wait_ge(stored, p * FFN * 16 + FFN * 16)

            pool.memset(neg_half[:], -0.5).then_inc(norm_consts, 1)
            pool.memset(eps_row[:], EPS).then_inc(norm_consts, 1)
            pool.dma_start(ident8[:], eye).then_inc(ident8_in, 16)
            load_masks(0)
            pool.wait_ge(norm_consts, 2)
            power(0, 0, NT)
            pool.wait_ge(consts_in, 112)
            pool.wait_ge(b2_in, 16)
            for l in range(L):
                n = step(pool.tensor_tensor(row_s[:, l, 1], row_s[:, l, 1], e[:, 0, l], ALU.add))
            split_chunks(0, 0, 0, CHUNKS)
            power(0, 0, NT)
            pool.wait_ge(pool_step, steps[0])
            with pool.Fori(0, PAIRS - 1) as p:
                pair(p, False)
            pair(PAIRS - 1, True)

        @block.vector
        def _(dve):
            steps = [0]
            norms = [0]
            aggs = [0]

            def step(ins):
                steps[0] += 1
                ins.then_inc(dve_step, 1)
                return steps[0]

            def need(n):
                dve.wait_ge(dve_step, n)

            def ask_rstd(tiles):
                ns = [step(dve.bn_stats(stats[:, t, :], src)) for t, src in tiles]
                for (t, _), n in zip(tiles, ns):
                    need(n)
                    ins = dve.bn_aggr(mv[:, t, :], stats[:, t, :])
                ins.then_inc(var_ready, 1)
                norms[0] += 1
                return norms[0]

            def normalise(dst, src, t):
                return dve.tensor_scalar(dst, src, mv[:, t, 0:1], rstd[:, t:t + 1], ALU.subtract, ALU.mult)

            def dots(l, b, t):
                for which, col in ((0, si), (1, sj)):
                    if steps[0] >= 2:
                        need(steps[0] - 1)
                    n = step(dve.tensor_tensor_reduce(junk[:, which, 0:D], X[b][:, t, 0:D], attn_row[:, l, which],
                                                      1.0, 0.0, ALU.mult, ALU.add, col[:, b, t:t + 1]))
                return n

            def graph_stats(q, b, t0, t1):
                if t0 == 0:
                    dve.wait_ge(x_loaded[b], q * 16 + 16)
                if t1 == NT:
                    ask_rstd([(t, X[b][:, t, 0:D]) for t in range(t0, t1)])
                else:
                    ns = [step(dve.bn_stats(stats[:, t, :], X[b][:, t, 0:D])) for t in range(t0, t1)]
                    for t, n in zip(range(t0, t1), ns):
                        need(n)
                        step(dve.bn_aggr(mv[:, t, :], stats[:, t, :]))

            def start_graph(p, q, b):
                dve.wait_ge(mask_loaded[b], q * 32 + 32)
                for t in range(NT):
                    own = mask[b][:, t, t * P:(t + 1) * P]
                    step(dve.tensor_tensor(own, own, ident8[:], ALU.add))
                dve.wait_ge(rstd_ready, p * NORMS + norms[0])
                for t in range(NT):
                    n = step(normalise(X[b][:, t, 0:D], X[b][:, t, 0:D], t))
                need(n)

            def first_dots(p, b, k, u=None):
                for t in range(NT):
                    n = dots(0, b, t)
                    if u is not None and t % 2:
                        beside_hidden(p, u, t // 2)
                need(n)
                dve.tensor_scalar(sj2[:, b], sj[:, b], SLOPE, None, ALU.mult).then_inc(s_ready, 1)
                dve.wait_ge(s_ready, p * PREPS + k + 1)

            def prepare(p, k):
                l, b = k % PREPS // 2, k % 2
                dve.wait_ge(work_moved, p * WORK + s_tile_end[k] + WORK_BUFS)
                need(step(dve.tensor_reduce(smin[:], s_row[:], AX.X, ALU.min)))
                need(step(dve.tensor_scalar(s_row[:], s_row[:], smin[:], 1.0, ALU.subtract, ALU.add)))
                for t in range(NT):
                    n = step(dve.tensor_tensor_reduce(junk[:, t % 2], nbr[b][:, t], s_row[:], 1.0, 0.0, ALU.mult, ALU.max,
                                                      u_col[:, t:t + 1]))
                    need(n - 1)
                need(n)
                need(step(dve.tensor_scalar(u_col[:], u_col[:], -1.0, smin[:], ALU.add, ALU.add)))
                need(step(dve.tensor_tensor(u_col[:], u_col[:], sj[:, b], ALU.max)))
                need(step(dve.tensor_scalar(c_col[:], si[:, b], attn_bias[:, l:l + 1], None, ALU.add)))
                need(step(dve.tensor_tensor(u_col[:], u_col[:], c_col[:], ALU.add)))
                need(step(dve.scalar_tensor_tensor(m_col[:], u_col[:], SLOPE, u_col[:], ALU.mult, ALU.max)))
                step(dve.tensor_tensor(G[:, b], c_col[:], m_col[:], ALU.subtract))
                dve.scalar_tensor_tensor(H[:, b], c_col[:], SLOPE, m_col[:], ALU.mult, ALU.subtract).then_inc(cols_ready, 1)

            def probabilities(p, g, t0, t1):
                l, b, half = unit(g)
                for t in range(t0, t1):
                    dve.wait_ge(exps_done, p * PT + g * NT + t + 1)
                    need(step(dve.tensor_tensor(prob[:, g % 2, t], prob[:, g % 2, t], branch[:, t], ALU.max)))
                    dve.tensor_tensor(prob[:, g % 2, t], prob[:, g % 2, t], mask[b][:, t, half * U:(half + 1) * U], ALU.min)\
                        .then_inc(prob_ready, 1)

            def first_norm(p, g, r, t0, t1):
                l, b, half = unit(g)
                bank = agg[aggs[0] % AGG_BUFS]
                dve.wait_ge(agg_done, p * AGG + aggs[0] + 1)
                if r == 0 and g >= 1:
                    dve.wait_ge(turn_done, p * GNN * KD + g * KD)
                    dve.wait_ge(hb_ready, p * GNN * UR + g * UR)
                need(step(dve.reciprocal(rden[:, r], bank[:, D:D + 1])))
                dve.scalar_tensor_tensor(h[:, r], bank[:, 0:D], rden[:, r], X[b][:, half * UR + r, 0:D], ALU.mult, ALU.add)\
                    .then_inc(agg_moved, 1)
                aggs[0] += 1
                dve.wait_ge(agg_moved, p * AGG + aggs[0] + AGG_BUFS)
                asked = ask_rstd([(r, h[:, r])])
                probabilities(p, g + 1, t0, t1)
                dve.wait_ge(rstd_ready, p * NORMS + asked)
                normalise(h[:, r], h[:, r], r).then_inc(h_ready, 1)

            def hT_half(p, g):
                dve.wait_ge(hT_full, p * GNN * KD + (g + 1) * KD)
                dve.tensor_tensor(inT[:, 1, 1], hT32[:, 1], inT[:, 0, 1], ALU.subtract).then_inc(hT_low[1], 1)

            def second_norm(p, g, t0, t1):
                l, b, half = unit(g)
                dve.wait_ge(hid_used, p * HIDS + (g + 1) * KH + HID_BUFS)
                dve.wait_ge(hb_ready, p * GNN * UR + (g + 1) * UR)
                for r in range(UR):
                    ins = dve.scalar_tensor_tensor(e[:, g % 2, r], ff[r // 2][:, r % 2 * D:(r % 2 + 1) * D], 1.0 / W_SCALE,
                                                   e[:, g % 2, r], ALU.mult, ALU.add)
                    if r < UR - 1:
                        step(ins)
                ins.then_inc(ff_moved, 1)
                dve.wait_ge(ff_moved, p * UNITS + g + 2)
                asked = ask_rstd([(UR + r, e[:, g % 2, r]) for r in range(UR)])
                if g + 1 < GNN:
                    hT_half(p, g + 1)
                probabilities(p, g + 2, t0, t1)
                dve.wait_ge(rstd_ready, p * NORMS + asked)
                for r in range(UR):
                    normalise(e[:, g % 2, r], e[:, g % 2, r], UR + r).then_inc(z_ready, 1)

            def hid_half(p, u, k):
                dve.wait_ge(hid_high, p * HIDS + u * KH + k + 1)
                dve.tensor_tensor(hid[:, k % HID_BUFS, 1], hid32[:, k % 2], hid[:, k % HID_BUFS, 0], ALU.subtract)\
                    .then_inc(hid_low[0], 1)

            def second_dots(p, g):
                l, b, half = unit(g)
                for r in range(UR):
                    if 2 + r < BY_DVE:
                        hid_half(p, g + 1, 2 + r)
                    dve.wait_ge(x_ready, p * GNN * UR + g * UR + r + 1)
                    n = dots(l + 1, b, half * UR + r)
                if half == HALVES - 1:
                    need(n)
                    dve.tensor_scalar(sj2[:, b], sj[:, b], SLOPE, None, ALU.mult).then_inc(s_ready, 1)
                    dve.wait_ge(s_ready, p * PREPS + (l + 1) * 2 + b + 1)

            def front_sum(p, f):
                b, half = f % 2, f // 2
                a = half * UR
                dve.wait_ge(x_ready, p * GNN * UR + (GNN - 2 * HALVES + b * HALVES + half + 1) * UR)
                dve.wait_ge(xin_loaded, p * FFN * 16 + FFN * 16)
                dve.tensor_tensor(X[b][:, a:a + UR, 0:D], X[b][:, a:a + UR, 0:D], x_in[:, f], ALU.add).then_inc(x1_ready, 1)
                dve.wait_ge(x1_ready, p * FFN + f + 1)
                ask_rstd([(r, X[b][:, a + r, 0:D]) for r in range(UR)])

            def front(p, f):
                b, half = f % 2, f // 2
                a = half * UR
                dve.wait_ge(rstd_ready, p * NORMS + norms[0])
                rows = h if f else first_rows
                if f == 0:
                    dve.wait_ge(x_ready, p * GNN * UR + (GNN - 1) * UR)
                    dve.wait_ge(hT_low[0], p * GNN + GNN)
                if f == 1:
                    dve.wait_ge(turn_done, p * GNN * KD + GNN * KD)
                    dve.wait_ge(hb_ready, p * GNN * UR + GNN * UR)
                    dve.wait_ge(work_done, p * WORK + front_end[0])
                for r in range(UR):
                    n = step(normalise(rows[:, r], X[b][:, a + r, 0:D], r))
                need(n)
                asked = ask_rstd([(r, rows[:, r]) for r in range(UR)])
                dve.wait_ge(rstd_ready, p * NORMS + asked)
                for r in range(UR):
                    ins = normalise(e[:, 0, r], rows[:, r], r)
                    if r < UR - 1:
                        step(ins)
                ins.then_inc(front_ready, 1)

            def attention_out(p, f):
                for d in range(KD):
                    dve.wait_ge(agg_done, p * AGG + aggs[0] + 1)
                    dve.wait_ge(work_moved, p * WORK + front_end[f] + WORK_BUFS)
                    dve.scalar_tensor_tensor(xfT[:, d], agg[aggs[0] % AGG_BUFS][:, 0:U], ffn_col[:, 2, d:d + 1], xfT[:, d],
                                             ALU.add, ALU.add).then_inc(agg_moved, 1)
                    aggs[0] += 1
                dve.wait_ge(agg_moved, p * AGG + aggs[0] + AGG_BUFS)
                for d in range(KD):
                    n = step(dve.tensor_scalar(inT[:, 0, d], xfT[:, d], IN_SCALE, None, ALU.mult))
                for d in range(KD):
                    if d == 0:
                        need(n)
                    dve.scalar_tensor_tensor(inT[:, 1, d], xfT[:, d], IN_SCALE, inT[:, 0, d], ALU.mult, ALU.subtract)\
                        .then_inc(xaT_split, 1)

            def expert_out(p, f):
                dve.wait_ge(hid_used, p * HIDS + (GNN + f + 1) * KH + HID_BUFS)
                for d in range(KD):
                    ins = dve.tensor_scalar(yT[:, d], ff[d][:, 0:U], 1.0 / W_SCALE, exp_col[:, f // 2, KH + d:KH + d + 1],
                                            ALU.mult, ALU.add)
                    if d < KD - 1:
                        step(ins)
                ins.then_inc(ff_moved, 1)

            def last_out(p, f, r0, r1):
                for r in range(r0, r1):
                    dve.wait_ge(agg_done, p * AGG + aggs[0] + 1)
                    if r == 0 and f > 0:
                        dve.wait_ge(stored, p * FFN * 16 + f * 16)
                    dve.tensor_tensor(e[:, 1, r], agg[aggs[0] % AGG_BUFS][:, 0:D], next_row[:], ALU.add).then_inc(agg_moved, 1)
                    aggs[0] += 1

            def beside_hidden(p, u, k):
                if k < BY_DVE:
                    hid_half(p, u, k)
                if k == 0 and GNN + 1 <= u < GNN + FFN - 1:
                    front_sum(p, u - GNN + 1)
                if u > GNN and k in (2, 3):
                    last_out(p, u - GNN - 1, 2 * k - 4, 2 * k - 2)

            def pair(p, last):
                dve.sem_clear(dve_step)
                steps[0], norms[0], aggs[0] = 0, 2, 0
                start_graph(p, p, 1)
                for g in range(GNN):
                    l, b, half = unit(g)
                    made = P_PLAN[half if g else 1] if g + 1 < GNN else (0,) * (UR + 2)
                    for r in range(UR):
                        first_norm(p, g, r, made[r - 1] if r else 0, made[r])
                    if g >= 1:
                        second_norm(p, g - 1, made[UR - 1], made[UR])
                        for k in range(2):
                            hid_half(p, g, k)
                        if g == GNN - 1:
                            front_sum(p, 0)
                        if unit(g - 1)[0] + 1 < L:
                            second_dots(p, g - 1)
                        else:
                            for k in range(2, BY_DVE):
                                hid_half(p, g, k)
                        probabilities(p, g + 1, made[UR], made[UR + 1])
                    else:
                        hT_half(p, g)
                        probabilities(p, g + 1, made[UR - 1], made[UR])
                        first_dots(p, 1, 1, g)
                        probabilities(p, g + 1, made[UR], made[UR + 1])
                    if prep_after(g) is not None:
                        prepare(p, prep_after(g))
                front(p, 0)
                front_sum(p, 1)
                for f in range(FFN):
                    attention_out(p, f)
                    if f == 0:
                        second_norm(p, GNN - 1, 0, 0)
                    else:
                        expert_out(p, f - 1)
                    if f == FFN - 1 and not last:
                        first_dots(p, 0, PREPS, GNN + f)
                    else:
                        for k in range(4):
                            beside_hidden(p, GNN + f, k)
                    if f < FFN - 1:
                        front(p, f + 1)
                    if f == 2 and not last:
                        graph_stats(p + 1, 0, 0, NT)
                        start_graph(p, p + 1, 0)
                    if f == 3 and not last:
                        graph_stats(p + 1, 1, 0, NT // 2)
                        prepare(p, PREPS)
                expert_out(p, FFN - 1)
                if not last:
                    graph_stats(p + 1, 1, NT // 2, NT)
                last_out(p, FFN - 1, 0, UR)
                if not last:
                    probabilities(p, GNN, 0, NT)
                dve.wait_ge(dve_step, steps[0])

            for b in range(2):
                dve.memset(X[b][:, :, D:D + 1], 1.0).then_inc(ones_set, 1)
            dve.sem_inc(agg_moved, AGG_BUFS)
            dve.sem_inc(ff_moved, 1)
            dve.wait_ge(ident8_in, 16)
            dve.wait_ge(ones_set, 2)
            graph_stats(0, 0, 0, NT)
            start_graph(0, 0, 0)
            dve.wait_ge(attn_in, 48)
            first_dots(0, 0, 0)
            prepare(0, 0)
            graph_stats(0, 1, 0, NT)
            dve.wait_ge(consts_in, 112)
            dve.tensor_scalar(norm_col[:], norm_col[:], IN_SCALE, None, ALU.mult).then_inc(ones_set, 1)
            dve.wait_ge(ones_set, 3)
            probabilities(0, 0, 0, NT)
            dve.wait_ge(dve_step, steps[0])
            with dve.Fori(0, PAIRS - 1) as p:
                pair(p, False)
            pair(PAIRS - 1, True)

        @block.scalar
        def _(act):
            works = [0]
            tables = [0]

            def table(p, function):
                act.wait_ge(table_loaded, p * TABLES + tables[0] + 1)
                act.activation(act_tick[:], ident[:, 0:1], function).then_inc(table_loaded, 1)
                tables[0] += 1

            def branches(p, g):
                l, b, half = unit(g)
                act.wait_ge(bcast_done, p * GNN + g + 1)
                if g >= 2:
                    act.wait_ge(agg_done, p * AGG + (min(g, GNN) - 1) * UR)
                for t in range(NT):
                    act.activation(prob[:, g % 2, t], g_bc[:, 0:U], ACT.Exp, bias=sj[:, b, t:t + 1])
                    if g >= 1:
                        act.wait_ge(prob_ready, p * PT + (g - 1) * NT + t + 1)
                    act.activation(branch[:, t], h_bc[:, 0:U], ACT.Exp, bias=sj2[:, b, t:t + 1]).then_inc(exps_done, 1)

            def move(p, dst, **how):
                n = works[0]
                act.wait_ge(work_done, p * WORK + n + 1)
                act.activation(dst, work[n % WORK_BUFS][:, 0:U], **how).then_inc(work_moved, 1)
                works[0] += 1

            def hidden(p, u, k, bias):
                if u or k >= 2:
                    wait_low(act, p, u, k - 2)
                move(p, hid32[:, k % 2], func=ACT.Gelu, bias=bias, scale=1.0 / (W_SCALE * IN_SCALE))
                act.wait_ge(hid_used, p * HIDS + u * KH + k + 1)
                act.wait_ge(work_moved, p * WORK + works[0] + WORK_BUFS)
                act.activation(hid[:, k % HID_BUFS, 0], hid32[:, k % 2], ACT.Copy).then_inc(hid_high, 1)

            def turned(p, g):
                l = unit(g)[0]
                table(p, ACT.Gelu)
                for dst, done in ((inT[:, 0], hT_high), (hT32, hT_full)):
                    for d in range(KD):
                        act.wait_ge(turn_done, p * GNN * KD + g * KD + d + 1)
                        act.activation(dst[:, d], (g_bc, h_bc)[d][:, 0:U], ACT.Identity, scale=norm_col[:, l, 0, d:d + 1],
                                       bias=norm_col[:, l, 1, d:d + 1]).then_inc(done, 1)

            def s_rows(p, k):
                if k >= 1:
                    act.wait_ge(cols_ready, p * PREPS + k)
                for t in range(S_TILES):
                    move(p, s_row[:, t * U:(t + 1) * U], func=ACT.Copy)

            def front(p, f):
                for d in range(KD):
                    move(p, xfT[:, d], func=ACT.Copy)
                for d in range(KD):
                    move(p, nT[:, d], func=ACT.Identity, scale=ffn_col[:, 0, d:d + 1], bias=ffn_col[:, 1, d:d + 1])

            def output(p, f):
                for r in range(UR):
                    act.wait_ge(agg_moved, p * AGG + last_tile[f] + r + 1 + AGG_BUFS)
                    act.activation(e[:, 1, r], e[:, 1, r], ACT.Gelu).then_inc(o_gelu, 1)

            def pair(p, last):
                works[0], tables[0] = S_TILES, 0
                for g in range(GNN):
                    l, b, half = unit(g)
                    if g + 1 < GNN:
                        table(p, ACT.Exp)
                        branches(p, g + 1)
                    turned(p, g)
                    for k in range(KH):
                        if k == KH - 1 and g == GNN - 1:
                            front(p, 0)
                        hidden(p, g, k, b1s[:, l, k:k + 1])
                        if k == S_AT + 1 and prep_after(g) is not None:
                            s_rows(p, prep_after(g))
                for f in range(FFN):
                    for k in range(KH):
                        if k == KH - 1 and f + 1 < FFN:
                            front(p, f + 1)
                        hidden(p, GNN + f, k, exp_col[:, f // 2, k:k + 1])
                        if k == O_AT + 1 and f >= 1:
                            output(p, f - 1)
                        if k == NEXT_AT + 1 and f == FFN - 1 and not last:
                            s_rows(p, PREPS)
                if not last:
                    table(p, ACT.Exp)
                    branches(p, GNN)
                output(p, FFN - 1)

            act.sem_inc(work_moved, WORK_BUFS)
            act.sem_inc(table_loaded, 1)
            act.wait_ge(attn_in, 48)
            s_rows(0, 0)
            branches(0, 0)
            with act.Fori(0, PAIRS - 1) as p:
                pair(p, False)
            pair(PAIRS - 1, True)

        @block.tensor
        def _(pe):
            works = [0]
            aggs = [0]

            def work_bank(p):
                pe.wait_ge(work_moved, p * WORK + works[0] + 1)
                works[0] += 1
                return work[(works[0] - 1) % WORK_BUFS]

            def agg_bank(p):
                pe.wait_ge(agg_moved, p * AGG + aggs[0] + 1)
                aggs[0] += 1
                return agg[(aggs[0] - 1) % AGG_BUFS]

            def s_rows(p, k):
                b = k % 2
                pe.wait_ge(s_ready, p * PREPS + k + 1)
                for i in range(S_TILES):
                    bank = work_bank(p)
                    for t in range(UR):
                        col = sj[:, b, i * UR + t:i * UR + t + 1]
                        ins = pe.transpose(bank[:, t * P:(t + 1) * P], col.to_broadcast([P, P]), ident[:])
                    ins.then_inc(work_done, 1)

            def broadcast(p, g):
                l, b, half = unit(g)
                pe.wait_ge(cols_ready, p * PREPS + g // (2 * HALVES) * 2 + b + 1)
                if g >= 1:
                    pe.wait_ge(exps_done, p * PT + g * NT)
                    if 2 <= g:
                        pe.wait_ge(hT_full, p * GNN * KD + (g - 1) * KD)
                for bank, col in ((g_bc, G), (h_bc, H)):
                    for t in range(UR):
                        c = half * UR + t
                        ins = pe.transpose(bank[:, t * P:(t + 1) * P], col[:, b, c:c + 1].to_broadcast([P, P]), ident[:])
                ins.then_inc(bcast_done, 1)

            def aggregate(p, g):
                l, b, half = unit(g)
                for r in range(UR):
                    if r == B_AT[half if g else 1] and g + 1 < GNN:
                        broadcast(p, g + 1)
                    bank = agg_bank(p)
                    for t in range(NT):
                        if r == 0:
                            pe.wait_ge(prob_ready, p * PT + g * NT + t + 1)
                        ins = pe.matmul(bank[:, 0:D + 1], prob[:, g % 2, t, r * P:(r + 1) * P], X[b][:, t, :],
                                        start=(t == 0), stop=(t == NT - 1))
                    ins.then_inc(agg_done, 1)

            def turn(p, src):
                for d in range(KD):
                    bank = work_bank(p)
                    for r in range(UR):
                        ins = pe.transpose(bank[:, r * P:(r + 1) * P], src[:, r, d * P:(d + 1) * P], ident[:])
                    ins.then_inc(work_done, 1)

            def turn_h(p, g):
                if g + 1 < GNN:
                    pe.wait_ge(exps_done, p * PT + (g + 2) * NT)
                for d in range(KD):
                    for r in range(UR):
                        if d == 0:
                            pe.wait_ge(h_ready, p * GNN * UR + g * UR + r + 1)
                        ins = pe.transpose((g_bc, h_bc)[d][:, r * P:(r + 1) * P], h[:, r, d * P:(d + 1) * P], ident[:])
                    ins.then_inc(turn_done, 1)

            def front(p, f):
                pe.wait_ge(front_ready, p * FFN + f + 1)
                turn(p, h if f else first_rows)
                turn(p, e[:, 0])

            def hidden_high(p, slot, k, g=None):
                bank = work_bank(p)
                for d in range(KD):
                    if g is not None and k == 0:
                        pe.wait_ge(hT_high, p * GNN * KD + g * KD + d + 1)
                    for half in range(2):
                        pe.matmul(bank[:, 0:U], w1s[:, slot, half, d, k * P:(k + 1) * P], inT[:, 0, d],
                                  start=(half == 0 and d == 0), stop=False)
                return bank

            def hidden_low(slot, k, bank):
                for d in range(KD):
                    ins = pe.matmul(bank[:, 0:U], w1s[:, slot, 0, d, k * P:(k + 1) * P], inT[:, 1, d],
                                    start=False, stop=(d == KD - 1))
                ins.then_inc(work_done, 1)

            def hidden(p, slot, k):
                hidden_low(slot, k, hidden_high(p, slot, k))

            def first_hidden(p, slot, g):
                banks = [hidden_high(p, slot, k, g) for k in range(2)]
                for d in range(KD):
                    pe.wait_ge(hT_low[d], p * GNN + g + 1)
                for k in range(2):
                    hidden_low(slot, k, banks[k])

            def sums(p, u, k):
                if k == 0:
                    pe.wait_ge(ff_moved, p * UNITS + u + 1)
                wait_low(pe, p, u, k)
                halves = ((0, 0), (0, 1), (1, 0))
                if u < GNN:
                    slot = unit(u)[0] % W_SLOTS
                    for r in range(UR):
                        for i, j in halves:
                            ins = pe.matmul(ff[r // 2][:, r % 2 * D:(r % 2 + 1) * D], hid[:, k % HID_BUFS, i, r * P:(r + 1) * P],
                                            w2s[:, slot, j, k], start=(k == 0 and r % 2 == 0 and i + j == 0),
                                            stop=(k == KH - 1 and i == 1), skip_group_check=True)
                else:
                    slot = (L + (u - GNN) // 2) % W_SLOTS
                    for d in range(KD):
                        for i, j in halves:
                            ins = pe.matmul(ff[d][:, 0:U], w2s[:, slot, j, k, d * P:(d + 1) * P], hid[:, k % HID_BUFS, i],
                                            start=(k == 0 and i + j == 0), stop=(k == KH - 1 and i == 1))
                ins.then_inc(hid_used, 1)

            def tail(p, u):
                for k in range(KH - TAIL, KH):
                    sums(p, u, k)

            def last_product(p, f, r0, r1):
                if r0 == 0:
                    pe.wait_ge(ff_moved, p * UNITS + GNN + f + 2)
                for r in range(r0, r1):
                    bank = agg_bank(p)
                    for c in range(KD):
                        ins = pe.matmul(bank[:, 0:D], yT[:, c, r * P:(r + 1) * P], next_ws[:, c], start=(c == 0), stop=(c == KD - 1))
                    ins.then_inc(agg_done, 1)

            def pair(p, last):
                works[0], aggs[0] = S_TILES, 0
                for g in range(GNN):
                    l, b, half = unit(g)
                    aggregate(p, g)
                    if g >= 1:
                        tail(p, g - 1)
                    turn_h(p, g)
                    if g % (2 * HALVES) == 0:
                        pe.wait_ge(w_split, p * PAIR_CHUNKS + FIRST_CHUNKS + l * CHUNKS)
                    first_hidden(p, l % W_SLOTS, g)
                    for k in range(2, KH):
                        if k == KH - 1 and g == GNN - 1:
                            front(p, 0)
                        hidden(p, l % W_SLOTS, k)
                        if k == S_AT + 1 and prep_after(g) is not None:
                            s_rows(p, prep_after(g))
                        if LAG <= k < KH - TAIL + LAG:
                            sums(p, g, k - LAG)
                for f in range(FFN):
                    stage = L + f // 2
                    if f % 2 == 0:
                        pe.wait_ge(w_split, p * PAIR_CHUNKS + FIRST_CHUNKS + stage * CHUNKS)
                        pe.wait_ge(exp_in[f // 2], p * 16 + 16)
                    pe.wait_ge(work_moved, p * WORK + front_end[f] + WORK_BUFS)
                    for d in range(KD):
                        bank = agg_bank(p)
                        for c in range(KD):
                            ins = pe.matmul(bank[:, 0:U], attn_ws[:, c, d * P:(d + 1) * P], nT[:, c], start=(c == 0), stop=(c == KD - 1))
                        ins.then_inc(agg_done, 1)
                    tail(p, GNN + f - 1)
                    pe.wait_ge(xaT_split, p * FFN * KD + (f + 1) * KD)
                    for k in range(KH):
                        if k == KH - 1 and f + 1 < FFN:
                            front(p, f + 1)
                        hidden(p, stage % W_SLOTS, k)
                        if k in (2, 3) and f >= 1:
                            last_product(p, f - 1, 2 * k - 4, 2 * k - 2)
                        if k == NEXT_AT + 1 and f == FFN - 1 and not last:
                            s_rows(p, PREPS)
                        if LAG <= k < KH - TAIL + LAG:
                            sums(p, GNN + f, k - LAG)
                tail(p, UNITS - 1)
                if not last:
                    broadcast(p, GNN)
                last_product(p, FFN - 1, 0, UR)

            pe.sem_inc(hid_used, HID_BUFS)
            pe.wait_ge(attn_in, 48)
            s_rows(0, 0)
            broadcast(0, 0)
            with pe.Fori(0, PAIRS - 1) as p:
                pair(p, False)
            pair(PAIRS - 1, True)


def kernel(**inputs):
    import numpy as np
    import concourse.bacc as bacc
    from concourse.bass_utils import run_bass_kernel_spmd

    a = {k: np.asarray(v) for k, v in inputs.items()}
    B, N, D = a["x"].shape
    L, E = a["L0_gnn_W1"].shape[0], a["L0_ffn_fc1_w"].shape[0]
    HID = a["L0_gnn_W1"].shape[2]

    def tiled(w):
        return np.moveaxis(w.reshape(*w.shape[:-2], w.shape[-2] // P, P, w.shape[-1]), -2, -3)

    def columns(v):
        return np.swapaxes(v.reshape(*v.shape[:-1], v.shape[-1] // P, P), -1, -2)

    arrays = {
        "x": tiled(a["x"]),
        "adj": tiled(a["adj"]),
        "adj_t": tiled(np.swapaxes(a["adj"], 1, 2)),
        "attn_rows": a["L0_gnn_attn_w"].reshape(L, 2, D),
        "attn_b": a["L0_gnn_attn_b"],
        "w1": tiled(a["L0_gnn_W1"]),
        "b1": np.moveaxis(columns(a["L0_gnn_b1"]), 0, 1),
        "w2": tiled(a["L0_gnn_W2"]),
        "b2_rows": a["L0_gnn_b2"],
        "rows": np.stack([a[f"L0_gnn_{n}"] for n in ("g1", "beta1", "g2", "beta2")], 1),
        "norm_cols": np.moveaxis(columns(np.stack([a["L0_gnn_g1"], a["L0_gnn_beta1"]], 1)), 2, 0),
        "ffn_cols": np.moveaxis(columns(np.stack([a[f"L0_ffn_{n}"] for n in ("ln_g", "ln_b", "attn_b")])), 0, 1),
        "attn_w": tiled(a["L0_ffn_attn_w"].T),
        "fc1": tiled(np.swapaxes(a["L0_ffn_fc1_w"], 1, 2)),
        "fc2": tiled(np.swapaxes(a["L0_ffn_fc2_w"], 1, 2)),
        "expert_cols": np.concatenate([columns(a["L0_ffn_fc1_b"]), columns(a["L0_ffn_fc2_b"])], 2),
        "next_w": tiled(a["L0_ffn_next_w"].T),
        "next_b": a["L0_ffn_next_b"],
        "eye": np.eye(P, dtype=np.float32),
    }
    arrays = {k: np.ascontiguousarray(v) for k, v in arrays.items()}
    nc = bacc.Bacc("TRN2", target_bir_lowering=False, num_devices=1)
    args = [nc.dram_tensor(f"in_{k}", v.shape, mybir.dt.from_np(v.dtype), kind="ExternalInput").ap() for k, v in arrays.items()]
    out = nc.dram_tensor("out", arrays["x"].shape, F32, kind="ExternalOutput").ap()
    adj_ffn_kernel(nc, *args, out)
    r = run_bass_kernel_spmd(nc, [{f"in_{k}": v for k, v in arrays.items()}], core_ids=[0])
    return np.moveaxis(r.results[0]["out"], 1, 2).reshape(B, N, D)
```
